# Optimizing a Trainium2 kernel written in Bass

```python
import numpy as np
import jax
import jax.numpy as jnp

def _softmax(x, axis=-1):
    return jax.nn.softmax(x, axis=axis)
def _gelu(x):
    return jax.nn.gelu(x, approximate=True)
def _silu(x):
    return jax.nn.silu(x)
def _sigmoid(x):
    return jax.nn.sigmoid(x)
def _layernorm(x, axis=-1, eps=1e-5):
    m = jnp.mean(x, axis=axis, keepdims=True)
    v = jnp.var(x, axis=axis, keepdims=True)
    return (x - m) / jnp.sqrt(v + eps)
def _scatter_add(tgt, idx, src, axis=0):
    return tgt.at[idx].add(src)
def _segment_sum(src, seg, n):
    return jax.ops.segment_sum(src, seg, n)

kernel_name = 'mk_conv_seq_d1_conv_nhwc768_752565'

def setup_inputs(seed: int = 0):
    np.random.seed(seed)
    _w = jnp.asarray
    def _rec_inputs():
        import jax
        import jax.numpy as jnp
        _gk = jax.random.key(seed)
        x = -4.65e-05 + 0.9999 * jax.random.normal(jax.random.fold_in(_gk, 1), (16, 64, 64, 768), jnp.float32)
        return x
    x = _rec_inputs()
    def _L0_conv_setup():
        import jax, jax.numpy as jnp
        import numpy as np
        RATE = 0.25

        def _low_mask(w, h):
            line = int((w * h * RATE) ** 0.5 // 2)
            m = np.zeros((w, h), dtype=np.float32)
            m[w // 2 - line:w // 2 + line, h // 2 - line:h // 2 + line] = 1.0
            return jnp.asarray(m)

        def fft_low(x):
            xb = jnp.transpose(x, (0, 3, 2, 1))
            w, h = (xb.shape[-2], xb.shape[-1])
            mask = _low_mask(w, h)
            fft = jnp.fft.fftshift(jnp.fft.fft2(xb, norm='forward'), axes=(-2, -1))
            fft = fft * mask
            inv = jnp.fft.ifft2(jnp.fft.ifftshift(fft, axes=(-2, -1)), norm='forward').real
            inv = jnp.abs(inv)
            return jnp.transpose(inv, (0, 3, 2, 1))
        key = jax.random.key(seed)
        k_x, k_w1, k_b1, k_w2, k_b2 = jax.random.split(key, 5)
        B, H, W, C = (16, 64, 64, 768)
        Dh = int(C * 0.25)
        s1 = 1.0 / np.sqrt(C)
        s2 = 1.0 / np.sqrt(Dh)
        return {'x': jax.random.normal(k_x, (B, H, W, C), dtype=jnp.float32), 'W1': jax.random.uniform(k_w1, (Dh, C), jnp.float32, -s1, s1), 'b1': jax.random.uniform(k_b1, (Dh,), jnp.float32, -s1, s1), 'W2': jax.random.uniform(k_w2, (C, Dh), jnp.float32, -s2, s2), 'b2': jax.random.uniform(k_b2, (C,), jnp.float32, -s2, s2)}
    _L0_conv_all = _L0_conv_setup()
    _L0_conv_in = {k: v for k, v in _L0_conv_all.items() if k in ('W1', 'b1', 'W2', 'b2', )}
    del _L0_conv_all

    return {
        "x": x,
        "L0_conv_W1": _L0_conv_in["W1"],
        "L0_conv_b1": _L0_conv_in["b1"],
        "L0_conv_W2": _L0_conv_in["W2"],
        "L0_conv_b2": _L0_conv_in["b2"],
    }

def reference(x, L0_conv_W1, L0_conv_b1, L0_conv_W2, L0_conv_b2):
    import jax
    import jax.numpy as jnp
    def _L0_conv_ref(x, W1, b1, W2, b2):
        import jax, jax.numpy as jnp
        import numpy as np
        RATE = 0.25

        def _low_mask(w, h):
            line = int((w * h * RATE) ** 0.5 // 2)
            m = np.zeros((w, h), dtype=np.float32)
            m[w // 2 - line:w // 2 + line, h // 2 - line:h // 2 + line] = 1.0
            return jnp.asarray(m)

        def fft_low(x):
            xb = jnp.transpose(x, (0, 3, 2, 1))
            w, h = (xb.shape[-2], xb.shape[-1])
            mask = _low_mask(w, h)
            fft = jnp.fft.fftshift(jnp.fft.fft2(xb, norm='forward'), axes=(-2, -1))
            fft = fft * mask
            inv = jnp.fft.ifft2(jnp.fft.ifftshift(fft, axes=(-2, -1)), norm='forward').real
            inv = jnp.abs(inv)
            return jnp.transpose(inv, (0, 3, 2, 1))
        xs = jnp.einsum('bhwc,dc->bhwd', x, W1) + b1
        xs = jax.nn.gelu(xs, approximate=False)
        xs = fft_low(xs)
        xs = jnp.einsum('bhwd,cd->bhwc', xs, W2) + b2
        return x + xs

    def _gn(v, G=32, eps=1e-5):
        B_, H_, W_, C_ = v.shape
        g = v.reshape(B_, H_, W_, G, C_ // G)
        m = jnp.mean(g, axis=(1, 2, 4), keepdims=True)
        s = jnp.var(g, axis=(1, 2, 4), keepdims=True)
        return ((g - m) / jnp.sqrt(s + eps)).reshape(v.shape)

    def _ln_c(v, eps=1e-6):
        m = jnp.mean(v, axis=-1, keepdims=True)
        s = jnp.var(v, axis=-1, keepdims=True)
        return (v - m) / jnp.sqrt(s + eps)

    def _ln_t(v, eps=1e-5):
        m = jnp.mean(v, axis=-1, keepdims=True)
        s = jnp.var(v, axis=-1, keepdims=True)
        return (v - m) / jnp.sqrt(s + eps)

    def _to_tokens(v):
        B_, H_, W_, C_ = v.shape
        return v.reshape(B_, H_ * W_, C_)
    def _from_tokens(t, like):
        return t.reshape(like.shape)

    x = _L0_conv_ref(x, L0_conv_W1, L0_conv_b1, L0_conv_W2, L0_conv_b2)
    return x


_drawn_inputs = setup_inputs


def setup_inputs(seed=0):
    import zlib

    import numpy as np

    out = dict(_drawn_inputs(seed))
    spreads = {}
    factors = {'L0_conv_b1': 8.0}
    for name, (base, spread) in spreads.items():
        noise = np.random.default_rng([zlib.crc32(name.encode()), seed]).standard_normal(out[name].shape)
        drawn = base * np.exp(spread * noise) if base else spread * noise
        out[name] = jnp.asarray(drawn.astype(out[name].dtype))
    for name, factor in factors.items():
        out[name] = (out[name] * factor).astype(out[name].dtype)
    return out
```

```python
from contextlib import ExitStack

import concourse.bass as bass
from concourse import mybir

F32 = mybir.dt.float32
F32R = mybir.dt.float32r
ALU = mybir.AluOpType
ACT = mybir.ActivationFunctionType

P = 128
IMAGES, H, W, C, D = 16, 64, 64, 768, 192
KC = C // P
TILES = H * W // P
PAIRS = TILES // 2
GROUP = 4
GROUPS = TILES // GROUP
DB = D - P
HALF = C // 2

BLOCKS = 4
UNITS = TILES * KC // BLOCKS
UPP = UNITS // PAIRS
XT_SLOTS = 4
AHEAD = 2

LAG = 6
HALVES = 2 * TILES

CHUNK = 8
CHUNKS = W // 2 // CHUNK
COLS_LOADS = 16 * 6
YBANKS = 3


def lowpass_kernel(nc, x, w1t, b1, w2t, b2, identity, filter_w, filter_h, corner_in, corner_out, out):
    x_v = x.rearrange("b h w c -> b (h w) c").rearrange("b (t p) c -> b p t c", p=P)
    out_v = out.rearrange("b h w c -> b (h w) c").rearrange("b (t p) c -> b p t c", p=P)
    rows = nc.dram_tensor("filtered_rows", (H, W, D), F32, kind="Internal").ap()
    rows_in = rows.rearrange("(t a) w d -> (a w) t d", a=2)

    ctx = ExitStack()
    with ctx:
        def sb(name, shape, dt=F32):
            return ctx.enter_context(nc.sbuf_tensor(name, shape, dt))

        def sem(name):
            return ctx.enter_context(nc.semaphore(name))

        xs = sb("xs", [P, TILES, C])
        w1s = sb("w1s", [P, KC, 2 * D], F32R)
        w2a_hi = sb("w2a_hi", [P, C], F32R)
        w2a_lo = sb("w2a_lo", [P, C], F32R)
        w2b_hi = sb("w2b_hi", [P, C], F32R)
        w2b_lo = sb("w2b_lo", [P, C], F32R)
        ident = sb("ident", [P, P])
        b1_rows = sb("b1_rows", [P, D])
        fw_hi = sb("fw_hi", [P, P], F32R)
        fw_lo = sb("fw_lo", [P, P], F32R)
        fh = sb("fh", [P, P])
        corner_w = sb("corner_w", [P, 4])
        corner_hw = sb("corner_hw", [P, 4 * P], F32R)
        xt_hi = sb("xt_hi", [P, XT_SLOTS, BLOCKS * P], F32R)
        xt_lo = sb("xt_lo", [P, XT_SLOTS, BLOCKS * P], F32R)
        hid = sb("hid", [P, 2, 2, D])
        hid_hi = sb("hid_hi", [P, 2, 2, D], F32R)
        hid_lo = sb("hid_lo", [P, 2, 2, D], F32R)
        filt = sb("filt", [P, 2, 2, D])
        cols_a = sb("cols_a", [P, 2, CHUNK, P])
        cols_b = sb("cols_b", [P, 2, 4, 2 * DB])
        diff = sb("diff", [P, D])
        corner_acc = sb("corner_acc", [P, D])
        corner = sb("corner", [P, 2 * P], F32R)
        ya_hi = sb("ya_hi", [P, TILES, P], F32R)
        ya_lo = sb("ya_lo", [P, TILES, P], F32R)
        yb = sb("yb", [P, TILES, P], F32R)
        y_abs = sb("y_abs", [P, 2, 4 * P])
        yb1 = sb("yb1", [P, 2, GROUP, P], F32R)

        ps = [ctx.enter_context(nc.psum_tensor(f"ps{n}", [P, 512], F32)) for n in range(8)]
        ps_xt = ps[0:2]
        ps_h = ps[2:4]
        ps_f = ps[4]
        ps_o = ps[5:8]
        ps_corner = ps[3]
        ps_y = [ps[0:3], ps[5:8]]

        s_const = sem("const_loaded")
        s_setup = sem("setup_done")
        s_chain = sem("setup_chain")
        s_x = [sem(f"x_loaded{g}") for g in range(GROUPS)]
        s_t = sem("transposed")
        s_xhi = sem("xt_hi_ready")
        s_xlo = sem("xt_lo_ready")
        s_m1 = sem("mm1_unit_done")
        s_sum = sem("hid_summed")
        s_pre = sem("hid_pre_ready")
        s_gelu = sem("gelu_done")
        s_hlo = sem("hid_lo_ready")
        s_f = sem("filtered_w")
        s_fs = sem("filtered_staged")
        s_fw = [sem(f"rows_written{n}") for n in range(2)]
        s_cols = [sem(f"cols_loaded{n}") for n in range(2)]
        s_diff = sem("corner_diff")
        s_acc = sem("corner_acc_done")
        s_cmm = sem("corner_sums_done")
        s_chi = sem("corner_hi_ready")
        s_corner = sem("corner_ready")
        s_y = sem("y_bank_done")
        s_yhi = sem("y_hi_ready")
        s_ylo = sem("y_lo_ready")
        s_yb1 = sem("yb1_ready")
        s_o = sem("out_half_done")
        s_add = sem("out_half_added")
        s_out = [sem(f"stored{g}") for g in range(GROUPS)]

        block = ctx.enter_context(nc.Block())

        def y_columns(y, c, v):
            return y[:].rearrange("p t (a n) -> p (t a) n", a=4)[:, :, CHUNK * c + 4 * v:CHUNK * c + 4 * v + 4]

        def later(i):
            return not isinstance(i, int) or i > 0

        def steps(a, c):
            if a and c:
                return [(s - LAG if s >= LAG else None, s if s < PAIRS else None) for s in range(PAIRS + LAG)]
            return [(s if a else None, s if c else None) for s in range(PAIRS)]

        def turns(eng, turn):
            turn(0, True, False)
            with eng.Fori(1, IMAGES) as i:
                turn(i, True, True)
            turn(IMAGES, False, True)

        def unit_ahead(q, j):
            n = UPP * q + j + AHEAD
            return n if n < UNITS else None

        OUT_HALVES = [(0, 1), (2,), (3,)]

        @block.sync
        def _(sp):
            stage = xs[:, TILES - GROUP, :]
            sp.dma_start(xs[:, TILES - 2:TILES, :].rearrange("p t (k d) -> p (t k) d", d=D)[:, 0:KC, :],
                         w1t.rearrange("(k p) d -> p k d", p=P)).then_inc(s_const, 16)
            sp.dma_start(stage, w2t[0:P, :]).then_inc(s_const, 16)
            for r in range(2):
                sp.dma_start(xs[r * DB:(r + 1) * DB, TILES - GROUP + 1, :], w2t[P:D, :]).then_inc(s_const, 16)
            for r in (64, 96):
                sp.dma_start(xs[r:r + 1, TILES - GROUP - 1, :], b2.rearrange("(a c) -> a c", a=1)).then_inc(s_const, 16)
            sp.dma_start(b1_rows[:], b1.partition_broadcast(P)).then_inc(s_const, 16)
            sp.dma_start(ident[:], identity).then_inc(s_const, 16)
            sp.dma_start(xs[:, TILES - GROUP - 2, 0:P], filter_w).then_inc(s_const, 16)
            sp.dma_start(fh[:], filter_h).then_inc(s_const, 16)
            sp.dma_start(corner_w[:], corner_in).then_inc(s_const, 16)
            sp.dma_start(xs[:, TILES - GROUP - 2, P:5 * P], corner_out).then_inc(s_const, 16)

            def load_x(i, g):
                if later(i):
                    sp.wait_ge(s_out[g], 16 * i)
                sp.dma_start(xs[:, GROUP * g:GROUP * (g + 1), :], x_v[i, :, GROUP * g:GROUP * (g + 1), :]).then_inc(s_x[g], 16)

            def store(i, g):
                sp.wait_ge(s_add, HALVES * i + 2 * GROUP * (g + 1))
                sp.dma_start(out_v[i, :, GROUP * g:GROUP * (g + 1), :], xs[:, GROUP * g:GROUP * (g + 1), :]).then_inc(s_out[g], 16)

            def write_rows(i, q):
                sp.wait_ge(s_fs, PAIRS * i + q + 1)
                sp.dma_start(rows_in[:, 2 * q:2 * q + 2, :], filt[:, q % 2, :, :]).then_inc(s_fw[q % 2], 16)

            def read_cols(i, c):
                if c == 0:
                    for n in range(2):
                        sp.wait_ge(s_fw[n], 16 * PAIRS // 2 * (i + 1))
                if c >= 2 or later(i):
                    sp.wait_ge(s_y, YBANKS * (CHUNKS * i + c - 1))
                for w2 in range(2):
                    wc = w2 * W // 2 + CHUNK * c
                    hs = slice(w2 * H, (w2 + 1) * H)
                    sp.dma_start(cols_a[hs, c % 2, :, :], rows[:, wc:wc + CHUNK, 0:P]).then_inc(s_cols[c % 2], 16)
                    for v in range(2):
                        sp.dma_start(cols_b[hs, c % 2, :, v * DB:(v + 1) * DB],
                                     rows[:, wc + 4 * v:wc + 4 * v + 4, P:D]).then_inc(s_cols[c % 2], 16)

            def turn(i, a, c):
                if not c:
                    for g in range(GROUPS):
                        if g == GROUPS - 2:
                            sp.wait_ge(s_setup, 1)
                        load_x(i, g)
                for s, (q, r) in enumerate(steps(a, c)):
                    if r is not None and r % 2 == 1:
                        store(i - 1, r // 2)
                    if q is not None and q >= 1:
                        write_rows(i, q - 1)
                    if a and c and s % 2 == 0 and 2 <= s <= PAIRS:
                        load_x(i, s // 2 - 1)
                if a:
                    write_rows(i, PAIRS - 1)
                    for n in range(CHUNKS):
                        read_cols(i, n)

            turns(sp, turn)
            for g in range(GROUPS):
                sp.wait_ge(s_out[g], 16 * IMAGES)
            for n in range(2):
                sp.wait_ge(s_fw[n], 16 * PAIRS // 2 * IMAGES)

        @block.tensor
        def _(pe):
            pe.wait_ge(s_setup, 1)

            def transpose_unit(i, n):
                if n * BLOCKS % (GROUP * KC) == 0:
                    pe.wait_ge(s_x[n * BLOCKS // (GROUP * KC)], 16 * (i + 1))
                if n >= 2:
                    pe.wait_ge(s_xlo, UNITS * i + n - 1)
                elif n == 0 and later(i):
                    pe.wait_ge(s_yhi, YBANKS * CHUNKS * i)
                for b in range(BLOCKS):
                    t, k = divmod(BLOCKS * n + b, KC)
                    ins = nc.tensor.transpose(ps_xt[n % 2][:, b * P:(b + 1) * P], xs[:, t, k * P:(k + 1) * P], ident[:])
                ins.then_inc(s_t, 1)

            def mm1_unit(i, n):
                pe.wait_ge(s_xlo, UNITS * i + n + 1)
                for b in range(BLOCKS):
                    t, k = divmod(BLOCKS * n + b, KC)
                    if k == 0 and (t >= 2 or later(i)):
                        pe.wait_ge(s_pre, TILES * i + t - 1)
                    hi = xt_hi[:, n % XT_SLOTS, b * P:(b + 1) * P]
                    lo = xt_lo[:, n % XT_SLOTS, b * P:(b + 1) * P]
                    nc.tensor.matmul(ps_h[t % 2][:, 0:2 * D], hi, w1s[:, k, :], start=k == 0, stop=False)
                    ins = nc.tensor.matmul(ps_h[t % 2][:, D:2 * D], lo, w1s[:, k, 0:D], start=False, stop=k == KC - 1)
                ins.then_inc(s_m1, 1)

            def filter_w_pair(i, q):
                pe.wait_ge(s_hlo, PAIRS * i + q + 1)
                if q >= 1 or later(i):
                    pe.wait_ge(s_fs, PAIRS * i + q)
                hi, lo = (m[:, q % 2, :, :].rearrange("p t d -> p (t d)") for m in (hid_hi, hid_lo))
                nc.tensor.matmul(ps_f[:, 0:2 * D], fw_hi[:], hi, start=True, stop=False)
                nc.tensor.matmul(ps_f[:, 0:2 * D], fw_lo[:], hi, start=False, stop=False)
                nc.tensor.matmul(ps_f[:, 0:2 * D], fw_hi[:], lo, start=False, stop=True).then_inc(s_f, 1)

            def corner_sums(i):
                pe.wait_ge(s_acc, PAIRS * (i + 1))
                pe.wait_ge(s_pre, TILES * (i + 1))
                nc.tensor.matmul(ps_corner[0:4, 0:D], corner_w[:], corner_acc[:], start=True, stop=True).then_inc(s_cmm, 1)

            def filter_h_chunk(i, c):
                banks = ps_y[c % 2]
                pe.wait_ge(s_cols[c % 2], COLS_LOADS * CHUNKS // 2 * i + COLS_LOADS * (c // 2 + 1))
                if c == 0:
                    pe.wait_ge(s_corner, i + 1)
                    pe.wait_ge(s_xlo, UNITS * (i + 1))
                elif c == 1 and later(i):
                    pe.wait_ge(s_add, HALVES * i)
                elif c >= 2:
                    pe.wait_ge(s_yhi, YBANKS * CHUNKS * i + YBANKS * (c - 1))
                for v in range(2):
                    nc.tensor.matmul(banks[v][:], corner[:, 0:P], corner_hw[:], start=True, stop=False)
                    for m in range(4):
                        ins = nc.tensor.matmul(banks[v][:, m * P:(m + 1) * P], cols_a[:, c % 2, 4 * v + m, :], fh[:],
                                               start=False, stop=m == 3)
                    ins.then_inc(s_y, 1)
                nc.tensor.matmul(banks[2][:], corner[:, P:2 * P], corner_hw[:], start=True, stop=False)
                for m in range(4):
                    ins = nc.tensor.matmul(banks[2][:, m * P:(m + 1) * P], cols_b[:, c % 2, m, :], fh[:],
                                           start=False, stop=m == 3)
                ins.then_inc(s_y, 1)

            def out_half(i, u):
                t, f = divmod(u, 2)
                if u == 0:
                    pe.wait_ge(s_ylo, YBANKS * CHUNKS * (i + 1))
                if u >= 3:
                    pe.wait_ge(s_add, HALVES * i + u - 2)
                o = ps_o[u % 3][:, 0:HALF]
                n = slice(f * HALF, (f + 1) * HALF)
                nc.tensor.matmul(o, ya_hi[:, t, :], w2a_hi[:, n], start=True, stop=False)
                nc.tensor.matmul(o, ya_hi[:, t, :], w2a_lo[:, n], start=False, stop=False)
                nc.tensor.matmul(o, ya_lo[:, t, :], w2a_hi[:, n], start=False, stop=False)
                nc.tensor.matmul(o, yb[:, t, :], w2b_hi[:, n], start=False, stop=False)
                if u % (2 * GROUP) == 0:
                    pe.wait_ge(s_yb1, GROUPS * i + t // GROUP + 1)
                nc.tensor.matmul(o, yb1[:, t // GROUP % 2, t % GROUP, :], w2b_lo[:, n], start=False, stop=True).then_inc(s_o, 1)

            def turn(i, a, c):
                for q, r in steps(a, c):
                    for j in range(UPP):
                        if q is not None:
                            if q == 0 and j == 0:
                                for n in range(AHEAD):
                                    transpose_unit(i, n)
                            if unit_ahead(q, j) is not None:
                                transpose_unit(i, unit_ahead(q, j))
                            mm1_unit(i, UPP * q + j)
                            if j == 1 and q >= 1:
                                filter_w_pair(i, q - 1)
                        if r is not None:
                            for u in OUT_HALVES[j]:
                                out_half(i - 1, 4 * r + u)
                if a:
                    filter_w_pair(i, PAIRS - 1)
                    corner_sums(i)
                    for n in range(CHUNKS):
                        filter_h_chunk(i, n)

            turns(pe, turn)

        @block.scalar
        def _(act):
            def xt_hi_unit(i, n):
                act.wait_ge(s_t, UNITS * i + n + 1)
                if n >= XT_SLOTS or later(i):
                    act.wait_ge(s_m1, UNITS * i + n - XT_SLOTS + 1)
                nc.scalar.activation(xt_hi[:, n % XT_SLOTS, :], ps_xt[n % 2][:], ACT.Copy).then_inc(s_xhi, 1)

            def gelu_pair(i, q):
                act.wait_ge(s_pre, TILES * i + 2 * q + 2)
                if q >= 2 or later(i):
                    act.wait_ge(s_f, PAIRS * i + q - 1)
                pre = hid[:, q % 2, :, :]
                nc.scalar.activation(hid_hi[:, q % 2, :, :], pre, ACT.Gelu)
                nc.scalar.activation(pre, pre, ACT.Gelu).then_inc(s_gelu, 1)

            def stage_filtered(i, q):
                act.wait_ge(s_f, PAIRS * i + q + 1)
                if q >= 2 or later(i):
                    act.wait_ge(s_fw[q % 2], 16 * (PAIRS // 2 * i + q // 2))
                nc.scalar.activation(filt[:, q % 2, :, :].rearrange("p t d -> p (t d)"), ps_f[:, 0:2 * D], ACT.Copy).then_inc(s_fs, 1)

            def y_hi_bank(i, c, v):
                act.wait_ge(s_y, YBANKS * CHUNKS * i + YBANKS * c + v + 1)
                bank = ps_y[c % 2][v][:].rearrange("p (m n) -> p n m", m=4)
                n = YBANKS * c + v
                if n >= 2 or later(i):
                    act.wait_ge(s_ylo, YBANKS * CHUNKS * i + n - 1)
                nc.scalar.activation(y_abs[:, n % 2, :], ps_y[c % 2][v][:], ACT.Abs)
                if v < 2:
                    nc.scalar.activation(y_columns(ya_hi, c, v), bank, ACT.Abs).then_inc(s_yhi, 1)
                else:
                    nc.scalar.activation(y_columns(yb, c, 0)[0:DB], bank[0:DB], ACT.Abs)
                    nc.scalar.activation(y_columns(yb, c, 1)[DB:P], bank[DB:P], ACT.Abs).then_inc(s_yhi, 1)

            def yb1_group(i, g):
                if g == 0:
                    act.wait_ge(s_yhi, YBANKS * CHUNKS * (i + 1))
                    act.wait_ge(s_ylo, YBANKS * CHUNKS * (i + 1))
                if g >= 2:
                    act.wait_ge(s_o, HALVES * i + 2 * GROUP * (g - 1))
                src = yb[:, GROUP * g:GROUP * (g + 1), :].rearrange("p t (a c v m) -> p (t a) c v m", a=4, v=2, m=4)
                dst = yb1[:, g % 2, :, :].rearrange("p t (a c v m) -> p (t a) c v m", a=4, v=2, m=4)
                nc.scalar.activation(dst[0:DB, :, :, 0, :], src[0:DB, :, :, 0, :].bitcast(F32), ACT.Copy)
                nc.scalar.activation(dst[0:DB, :, :, 1, :], src[DB:P, :, :, 1, :].bitcast(F32), ACT.Copy).then_inc(s_yb1, 1)

            def turn(i, a, c):
                if c:
                    yb1_group(i - 1, 0)
                for q, r in steps(a, c):
                    for j in range(UPP):
                        if q is not None:
                            if q == 0 and j == 0:
                                for n in range(AHEAD):
                                    xt_hi_unit(i, n)
                            if unit_ahead(q, j) is not None:
                                xt_hi_unit(i, unit_ahead(q, j))
                            if q >= 1 and j == 0:
                                gelu_pair(i, q - 1)
                            if q >= 1 and j == 2:
                                stage_filtered(i, q - 1)
                        if r is not None and r % 2 == 0 and j == 1 and r // 2 + 1 < GROUPS:
                            yb1_group(i - 1, r // 2 + 1)
                if a:
                    gelu_pair(i, PAIRS - 1)
                    stage_filtered(i, PAIRS - 1)
                    for n in range(CHUNKS):
                        for v in range(YBANKS):
                            y_hi_bank(i, n, v)

            turns(act, turn)

        @block.vector
        def _(dve):
            chain = [0]

            def link(ins):
                chain[0] += 1
                ins.then_inc(s_chain, 1)
                dve.wait_ge(s_chain, chain[0])

            dve.wait_ge(s_const, 16 * 12)
            w1f = xs[:, TILES - 2:TILES, :].rearrange("p t (k d) -> p (t k) d", d=D)[:, 0:KC, :]
            w2af, w2bf, b2f = (xs[:, TILES - GROUP + n, :] for n in (0, 1, -1))
            fwf = xs[:, TILES - GROUP - 2, 0:P]
            nc.vector.memset(corner[:].bitcast(F32), 0.0)
            nc.vector.memset(w2b_lo[DB:P, :].bitcast(F32), 0.0)
            nc.vector.memset(yb1[DB:P, :, :, :].bitcast(F32), 1.0)
            nc.vector.tensor_copy(w1s[:, :, 0:D], w1f)
            nc.vector.tensor_copy(w2a_hi[:], w2af)
            nc.vector.tensor_copy(w2b_hi[:], w2bf)
            nc.vector.tensor_copy(corner_hw[:], xs[:, TILES - GROUP - 2, P:5 * P])
            link(nc.vector.tensor_copy(fw_hi[:], fwf))
            nc.vector.tensor_tensor(w1s[:, :, D:2 * D], w1f, w1s[:, :, 0:D].bitcast(F32), ALU.subtract)
            nc.vector.tensor_tensor(w2a_lo[:], w2af, w2a_hi[:].bitcast(F32), ALU.subtract)
            nc.vector.tensor_tensor(w2b_lo[0:DB, :], w2bf[0:DB], w2b_hi[0:DB, :].bitcast(F32), ALU.subtract)
            nc.vector.tensor_tensor(fw_lo[:], fwf, fw_hi[:].bitcast(F32), ALU.subtract)
            nc.vector.tensor_copy(w2b_lo[DB:DB + 1, :], b2f[DB:DB + 1])
            link(nc.vector.tensor_copy(w2b_lo[96:97, :], b2f[96:97]))
            nc.vector.tensor_tensor(w2b_lo[96:97, :], b2f[96:97], w2b_lo[96:97, :].bitcast(F32), ALU.subtract).then_inc(s_setup, 1)

            def xt_lo_unit(i, n):
                dve.wait_ge(s_xhi, UNITS * i + n + 1)
                nc.vector.tensor_tensor(xt_lo[:, n % XT_SLOTS, :], ps_xt[n % 2][:], xt_hi[:, n % XT_SLOTS, :].bitcast(F32),
                                        ALU.subtract).then_inc(s_xlo, 1)

            def hid_sum(i, t):
                dve.wait_ge(s_m1, UNITS * i + -(-KC * (t + 1) // BLOCKS))
                if t % 2 == 0 and (t >= 4 or later(i)):
                    dve.wait_ge(s_acc, PAIRS * i + t // 2 - 1)
                nc.vector.tensor_tensor(hid[:, t // 2 % 2, t % 2, :], ps_h[t % 2][:, D:2 * D], b1_rows[:], ALU.add).then_inc(s_sum, 1)

            def hid_pre(i, t):
                dve.wait_ge(s_sum, TILES * i + t + 1)
                h = hid[:, t // 2 % 2, t % 2, :]
                nc.vector.tensor_tensor(h, ps_h[t % 2][:, 0:D], h, ALU.add).then_inc(s_pre, 1)

            def hid_lo_pair(i, q):
                dve.wait_ge(s_gelu, PAIRS * i + q + 1)
                if q >= 2 or later(i):
                    dve.wait_ge(s_f, PAIRS * i + q - 1)
                nc.vector.tensor_tensor(hid_lo[:, q % 2, :, :], hid[:, q % 2, :, :], hid_hi[:, q % 2, :, :].bitcast(F32),
                                        ALU.subtract).then_inc(s_hlo, 1)

            def corner_split(i):
                dve.wait_ge(s_cmm, i + 1)
                nc.vector.tensor_copy(corner[0:4, 0:D], ps_corner[0:4, 0:D])
                nc.vector.tensor_copy(corner[0:4, D:2 * P], ps_corner[0:4, P:D]).then_inc(s_chi, 1)
                dve.wait_ge(s_chi, i + 1)
                nc.vector.tensor_tensor(corner[32:36, 0:D], ps_corner[0:4, 0:D], corner[0:4, 0:D].bitcast(F32), ALU.subtract)
                nc.vector.tensor_tensor(corner[32:36, D:2 * P], ps_corner[0:4, P:D], corner[0:4, D:2 * P].bitcast(F32),
                                        ALU.subtract).then_inc(s_corner, 1)

            def y_lo_bank(i, c, v):
                dve.wait_ge(s_yhi, YBANKS * CHUNKS * i + YBANKS * c + v + 1)
                bank = y_abs[:, (YBANKS * c + v) % 2, :].rearrange("p (m n) -> p n m", m=4)

                def lo(dst, src, hi):
                    return nc.vector.tensor_tensor(dst, src, hi.bitcast(F32), ALU.subtract)

                if v < 2:
                    lo(y_columns(ya_lo, c, v), bank, y_columns(ya_hi, c, v)).then_inc(s_ylo, 1)
                else:
                    lo(y_columns(yb, c, 0)[DB:P], bank[0:DB], y_columns(yb, c, 0)[0:DB])
                    lo(y_columns(yb, c, 1)[0:DB], bank[DB:P], y_columns(yb, c, 1)[DB:P]).then_inc(s_ylo, 1)

            def add_half(i, u):
                dve.wait_ge(s_o, HALVES * i + u + 1)
                t, f = divmod(u, 2)
                x_half = xs[:, t, f * HALF:(f + 1) * HALF]
                nc.vector.tensor_tensor(x_half, ps_o[u % 3][:, 0:HALF], x_half, ALU.add).then_inc(s_add, 1)

            def turn(i, a, c):
                for q, r in steps(a, c):
                    for j in range(UPP):
                        if q is not None:
                            if q == 0 and j == 0:
                                for n in range(AHEAD):
                                    xt_lo_unit(i, n)
                            if unit_ahead(q, j) is not None:
                                xt_lo_unit(i, unit_ahead(q, j))
                            if q >= 1 and j == 0:
                                hid_lo_pair(i, q - 1)
                            if j >= 1:
                                hid_sum(i, 2 * q + j - 1)
                                hid_pre(i, 2 * q + j - 1)
                        if r is not None:
                            for u in OUT_HALVES[j]:
                                add_half(i - 1, 4 * r + u)
                if a:
                    hid_lo_pair(i, PAIRS - 1)
                    corner_split(i)
                    for n in range(CHUNKS):
                        for v in range(YBANKS):
                            y_lo_bank(i, n, v)

            turns(dve, turn)

        @block.gpsimd
        def _(pool):
            def turn(i, a, c):
                if not a:
                    return
                for q in range(PAIRS):
                    pool.wait_ge(s_gelu, PAIRS * i + q + 1)
                    if q == 0:
                        if later(i):
                            pool.wait_ge(s_cmm, i)
                        nc.gpsimd.tensor_tensor(corner_acc[:], hid[:, 0, 0, :], hid[:, 0, 1, :], ALU.subtract).then_inc(s_acc, 1)
                        continue
                    pool.wait_ge(s_acc, PAIRS * i + q)
                    nc.gpsimd.tensor_tensor(diff[:], hid[:, q % 2, 0, :], hid[:, q % 2, 1, :], ALU.subtract).then_inc(s_diff, 1)
                    pool.wait_ge(s_diff, (PAIRS - 1) * i + q)
                    nc.gpsimd.tensor_tensor(corner_acc[:], corner_acc[:], diff[:], ALU.add).then_inc(s_acc, 1)

            turns(pool, turn)


def filters():
    import numpy as np

    n = np.arange(H)
    line = int((W * H * 0.25) ** 0.5 // 2)
    freq = np.arange(-line, line)
    d = n[:, None] - n[None, :]
    real = np.cos(2 * np.pi * freq[:, None, None] * d / H).sum(0) / H
    cos, sin = np.array([1, 0, -1, 0])[n % 4], np.array([0, 1, 0, -1])[n % 4]
    filter_w = np.kron(np.eye(2), real)
    filter_h = np.einsum("uv,hg->uhgv", np.eye(2), real).reshape(P, P)
    corner_in = np.zeros((2, W, 4))
    for a in range(2):
        corner_in[a, :, 2 * a] = cos / (H * W)
        corner_in[a, :, 2 * a + 1] = sin / (H * W)
    spread = np.zeros((P, 4, H, 2))
    for m in range(4):
        for w2 in range(2):
            terms = (-sin * sin[m], sin * cos[m], cos * sin[m], -cos * cos[m])
            for j, term in enumerate(terms):
                spread[j, m, :, w2] = spread[32 + j, m, :, w2] = term
    f = np.float32
    return {"identity": np.eye(P, dtype=f), "filter_w": filter_w.astype(f), "filter_h": filter_h.astype(f),
            "corner_in": corner_in.reshape(P, 4).astype(f), "corner_out": spread.reshape(P, 4 * P).astype(f)}


def kernel(x, L0_conv_W1, L0_conv_b1, L0_conv_W2, L0_conv_b2):
    import numpy as np
    import concourse.bacc as bacc
    from concourse.bass_utils import run_bass_kernel_spmd

    arrays = {
        "x": np.ascontiguousarray(x),
        "w1t": np.ascontiguousarray(np.asarray(L0_conv_W1).T),
        "b1": np.ascontiguousarray(L0_conv_b1),
        "w2t": np.ascontiguousarray(np.asarray(L0_conv_W2).T),
        "b2": np.ascontiguousarray(L0_conv_b2),
        **filters(),
    }
    nc = bacc.Bacc("TRN2", target_bir_lowering=False, num_devices=1, dynamic_dma_scratch_size=1024)
    aps = [nc.dram_tensor(f"{name}_dram", a.shape, mybir.dt.from_np(a.dtype), kind="ExternalInput").ap()
           for name, a in arrays.items()]
    out = nc.dram_tensor("out_dram", arrays["x"].shape, F32, kind="ExternalOutput").ap()
    lowpass_kernel(nc, *aps, out)
    result = run_bass_kernel_spmd(nc, [{f"{name}_dram": a for name, a in arrays.items()}], core_ids=[0])
    return result.results[0]["out_dram"]
```

```python
from contextlib import ExitStack

import concourse.bass as bass
from concourse import mybir

F32 = mybir.dt.float32
F32R = mybir.dt.float32r
ALU = mybir.AluOpType
ACT = mybir.ActivationFunctionType

P = 128
IMAGES, H, W, C, D = 16, 64, 64, 768, 192
KC = C // P
TILES = H * W // P
PAIRS = TILES // 2
GROUP = 4
GROUPS = TILES // GROUP
DB = D - P
HALF = C // 2

BLOCKS = 4
UNITS = TILES * KC // BLOCKS
UPP = UNITS // PAIRS
XT_SLOTS = 4
AHEAD = 2

LAG = 6
TAIL = 2 * GROUP
TAIL_PAIRS = TAIL // 2
FIRST_TAIL = TILES - TAIL
TAIL_STEPS = 13, 14
RELOAD_STEPS = 15, 17
HALVES = 2 * TILES

CHUNK = 8
CHUNKS = W // 2 // CHUNK
BCOLS = W // 4
BMULS = BCOLS // CHUNKS
YBANKS = 3


def lowpass_kernel(nc, x, w1t, b1, w2t, b2, identity, filter_w, filter_h, corner_in, corner_out, out):
    x_v = x.rearrange("b h w c -> b (h w) c").rearrange("b (t p) c -> b p t c", p=P)
    out_v = out.rearrange("b h w c -> b (h w) c").rearrange("b (t p) c -> b p t c", p=P)
    rows = nc.dram_tensor("filtered_rows", (H, W, D), F32, kind="Internal").ap()
    rows_in = rows.rearrange("(t a) w d -> (a w) t d", a=2)

    ctx = ExitStack()
    with ctx:
        def sb(name, shape, dt=F32):
            return ctx.enter_context(nc.sbuf_tensor(name, shape, dt))

        def sem(name):
            return ctx.enter_context(nc.semaphore(name))

        xs = sb("xs", [P, TILES, C])
        w1s = sb("w1s", [P, KC, 2 * D], F32R)
        w2a_hi = sb("w2a_hi", [P, C], F32R)
        w2a_lo = sb("w2a_lo", [P, C], F32R)
        w2b_hi = sb("w2b_hi", [P, C], F32R)
        w2b_lo = sb("w2b_lo", [P, C], F32R)
        ident = sb("ident", [P, P])
        b1_rows = sb("b1_rows", [P, D])
        fw_hi = sb("fw_hi", [P, P], F32R)
        fw_lo = sb("fw_lo", [P, P], F32R)
        fh = sb("fh", [P, P])
        corner_w = sb("corner_w", [P, 4])
        corner_hw = sb("corner_hw", [P, 4 * P], F32R)
        xt_hi = sb("xt_hi", [P, XT_SLOTS, BLOCKS * P], F32R)
        xt_lo = sb("xt_lo", [P, XT_SLOTS, BLOCKS * P], F32R)
        hid = sb("hid", [P, 2, 2, D])
        hid_hi = sb("hid_hi", [P, 2, 2, D], F32R)
        hid_lo = sb("hid_lo", [P, 2, 2, D], F32R)
        filt = sb("filt", [P, 2, 2, D])
        tail = sb("tail", [P, TAIL * C])
        x_tail = tail[:].rearrange("p (t c) -> p t c", c=C)
        cols_a = tail[:, 0:W // 2 * P].rearrange("p (m d) -> p m d", d=P)
        cols_b = tail[:, W // 2 * P:].rearrange("p (m d) -> p m d", d=2 * DB)
        diff = sb("diff", [P, D])
        corner_acc = sb("corner_acc", [P, D])
        corner = sb("corner", [P, 2 * P], F32R)
        ya = sb("ya", [P, TILES, P])
        yb = sb("yb", [P, 2 * H, BCOLS])
        oa_hi = sb("oa_hi", [P, 2, 2, P], F32R)
        oa_lo = sb("oa_lo", [P, 2, 2, P], F32R)
        ob = sb("ob", [P, 2, 2, P], F32R)
        ob1 = sb("ob1", [P, 2, 2, P], F32R)

        ps = [ctx.enter_context(nc.psum_tensor(f"ps{n}", [P, 512], F32)) for n in range(8)]
        ps_xt = ps[0:2]
        ps_h = ps[2:4]
        ps_f = ps[4]
        ps_o = [ps[6], ps[7], ps[5]]
        ps_corner = ps[3]
        ps_y = [ps[0:3], ps[3:6]]

        s_const = sem("const_loaded")
        s_ident = sem("ident_loaded")
        s_w1 = sem("w1_loaded")
        s_w1s = sem("w1_ready")
        s_setup = sem("setup_done")
        s_chain = sem("setup_chain")
        s_x = [sem(f"x_loaded{g}") for g in range(GROUPS)]
        s_t = sem("transposed")
        s_xhi = sem("xt_hi_ready")
        s_xlo = sem("xt_lo_ready")
        s_m1 = sem("mm1_unit_done")
        s_sum = sem("hid_summed")
        s_pre = sem("hid_pre_ready")
        s_gelu = sem("gelu_done")
        s_hlo = sem("hid_lo_ready")
        s_f = sem("filtered_w")
        s_fs = sem("filtered_staged")
        s_fw = [sem(f"rows_written{n}") for n in range(2)]
        s_cols_a = [sem(f"cols_a_loaded{c}") for c in range(CHUNKS)]
        s_cols_b = [sem(f"cols_b_loaded{n}") for n in range(2)]
        s_diff = sem("corner_diff")
        s_acc = sem("corner_acc_done")
        s_cmm = sem("corner_sums_done")
        s_chi = sem("corner_hi_ready")
        s_corner = sem("corner_ready")
        s_y = sem("y_bank_done")
        s_yabs = sem("y_bank_stored")
        s_ahi = sem("oa_hi_ready")
        s_bhi = sem("ob_hi_ready")
        s_alo = sem("oa_lo_ready")
        s_blo = sem("ob_lo_ready")
        s_b1 = sem("ob1_ready")
        s_xt = [sem(f"x_tail_loaded{n}") for n in range(TAIL // GROUP)]
        s_o = sem("out_half_done")
        s_add = sem("out_half_added")
        s_out = [sem(f"stored{g}") for g in range(GROUPS)]

        block = ctx.enter_context(nc.Block())

        def quarters(o, v):
            return o.rearrange("p t (n v m) -> p (t n) v m", v=2, m=BCOLS)[:, :, v, :]

        def yb_pair(r):
            return yb[:, 8 * r:8 * (r + 1), :]

        def later(i):
            return not isinstance(i, int) or i > 0

        def steps(a, c):
            if not a:
                return [(None, r) for r in range(PAIRS)]
            if not c:
                return [(q, None) for q in range(PAIRS + 1)]
            before = PAIRS - TAIL_PAIRS
            return ([(s - LAG if s >= LAG else None, s) for s in range(before)]
                    + [(q, None) for q in range(before - LAG, PAIRS)]
                    + [(PAIRS, before)] + [(None, r) for r in range(before + 1, PAIRS - 1)])

        def turns(eng, turn):
            turn(0, True, False)
            with eng.Fori(1, IMAGES) as i:
                turn(i, True, True)
            turn(IMAGES, False, True)

        def unit_ahead(q, j):
            n = UPP * q + j + AHEAD
            return n if n < UNITS else None

        def x_tile(t):
            return xs[:, t, :] if t < FIRST_TAIL else x_tail[:, t - FIRST_TAIL, :]

        OUT_HALVES = [(0, 1), (2,), (3,)]

        @block.sync
        def _(sp):
            def const(dst, src, s=s_const):
                sp.dma_start(dst, src).then_inc(s, 16)

            const(ident[:], identity, s_ident)
            const(x_tail[:, TAIL - 2:TAIL, :].rearrange("p t (k d) -> p (t k) d", d=D)[:, 0:KC, :],
                  w1t.rearrange("(k p) d -> p k d", p=P), s_w1)
            const(b1_rows[:], b1.partition_broadcast(P), s_w1)

            def load_constants():
                const(x_tail[:, 0, 0:P], filter_w)
                const(x_tail[:, 0, P:5 * P], corner_out)
                const(fh[:], filter_h)
                const(corner_w[:], corner_in)
                const(x_tail[:, 1, :], w2t[0:P, :])
                for r in range(2):
                    const(x_tail[r * DB:(r + 1) * DB, 2, :], w2t[P:D, :])
                for r in (64, 96):
                    const(x_tail[r:r + 1, 3, :], b2.rearrange("(a c) -> a c", a=1))

            def load_x(i, g):
                if later(i):
                    sp.wait_ge(s_out[g], 16 * i)
                sp.dma_start(xs[:, GROUP * g:GROUP * (g + 1), :], x_v[i, :, GROUP * g:GROUP * (g + 1), :]).then_inc(s_x[g], 16)

            def load_x_tail(i, n):
                if later(i):
                    sp.wait_ge(s_y, YBANKS * CHUNKS * i)
                else:
                    sp.wait_ge(s_setup, 1)
                sp.dma_start(x_tail[:, GROUP * n:GROUP * (n + 1), :],
                             x_v[i, :, FIRST_TAIL + GROUP * n:FIRST_TAIL + GROUP * (n + 1), :]).then_inc(s_xt[n], 16)

            def store(i, g):
                sp.wait_ge(s_add, HALVES * i + 2 * GROUP * (g + 1) + 1)
                sp.dma_start(out_v[i, :, GROUP * g:GROUP * (g + 1), :], xs[:, GROUP * g:GROUP * (g + 1), :]).then_inc(s_out[g], 16)

            def write_rows(i, q):
                sp.wait_ge(s_fs, PAIRS * i + q + 1)
                sp.dma_start(rows_in[:, 2 * q:2 * q + 2, :], filt[:, q % 2, :, :]).then_inc(s_fw[q % 2], 16)

            def read_cols_a(i, c):
                if c == 0:
                    for n in range(2):
                        sp.wait_ge(s_fw[n], 16 * PAIRS // 2 * (i + 1))
                for w2 in range(2):
                    wc = w2 * W // 2 + CHUNK * c
                    sp.dma_start(cols_a[w2 * H:(w2 + 1) * H, CHUNK * c:CHUNK * (c + 1), :],
                                 rows[:, wc:wc + CHUNK, 0:P]).then_inc(s_cols_a[c], 16)

            def read_cols_b(i, n):
                for w2 in range(2):
                    for v in range(2):
                        wc = w2 * W // 2 + v * BCOLS + n * BCOLS // 2
                        sp.dma_start(cols_b[w2 * H:(w2 + 1) * H, n * BCOLS // 2:(n + 1) * BCOLS // 2, v * DB:(v + 1) * DB],
                                     rows[:, wc:wc + BCOLS // 2, P:D]).then_inc(s_cols_b[n], 16)

            def turn(i, a, c):
                if not c:
                    for g in range(FIRST_TAIL // GROUP):
                        load_x(i, g)
                        if g == 0:
                            load_constants()
                        if g == 2:
                            for n in range(TAIL // GROUP):
                                load_x_tail(i, n)
                reload_steps = RELOAD_STEPS if a else (7, 8)
                for s, (q, r) in enumerate(steps(a, c)):
                    if r is not None and r % 2 == 1 and not (a and r == PAIRS - 3):
                        store(i - 1, r // 2)
                    if c and s in reload_steps:
                        load_x(i - 1, FIRST_TAIL // GROUP + reload_steps.index(s))
                    if q is not None and q >= 1:
                        write_rows(i, q - 1)
                    if a and c and s % 2 == 0 and 2 <= s <= PAIRS - TAIL_PAIRS:
                        load_x(i, s // 2 - 1)
                    if a and c and s in TAIL_STEPS:
                        load_x_tail(i, TAIL_STEPS.index(s))
                if a:
                    for n in range(2):
                        read_cols_a(i, 2 * n)
                        read_cols_b(i, n)
                        read_cols_a(i, 2 * n + 1)
                    if c:
                        store(i - 1, GROUPS - 2)
                        store(i - 1, GROUPS - 1)

            turns(sp, turn)
            for g in range(GROUPS):
                sp.wait_ge(s_out[g], 16 * IMAGES)
            for n in range(2):
                sp.wait_ge(s_fw[n], 16 * PAIRS // 2 * IMAGES)

        @block.tensor
        def _(pe):
            pe.wait_ge(s_ident, 16)

            def transpose_unit(i, n):
                if n * BLOCKS % (GROUP * KC) == 0:
                    g = n * BLOCKS // (GROUP * KC)
                    if g < FIRST_TAIL // GROUP:
                        pe.wait_ge(s_x[g], 16 * (i + 1))
                    else:
                        pe.wait_ge(s_xt[g - FIRST_TAIL // GROUP], 16 * (i + 1))
                if n >= 2:
                    pe.wait_ge(s_xlo, UNITS * i + n - 1)
                elif n == 0 and later(i):
                    pe.wait_ge(s_yabs, YBANKS * CHUNKS * i)
                for b in range(BLOCKS):
                    t, k = divmod(BLOCKS * n + b, KC)
                    ins = nc.tensor.transpose(ps_xt[n % 2][:, b * P:(b + 1) * P], x_tile(t)[:, k * P:(k + 1) * P], ident[:])
                ins.then_inc(s_t, 1)

            def mm1_unit(i, n):
                if n == 0 and not later(i):
                    pe.wait_ge(s_w1s, 1)
                pe.wait_ge(s_xlo, UNITS * i + n + 1)
                for b in range(BLOCKS):
                    t, k = divmod(BLOCKS * n + b, KC)
                    if k == 0 and (t >= 2 or later(i)):
                        pe.wait_ge(s_pre, TILES * i + t - 1)
                    hi = xt_hi[:, n % XT_SLOTS, b * P:(b + 1) * P]
                    lo = xt_lo[:, n % XT_SLOTS, b * P:(b + 1) * P]
                    nc.tensor.matmul(ps_h[t % 2][:, 0:2 * D], hi, w1s[:, k, :], start=k == 0, stop=False)
                    ins = nc.tensor.matmul(ps_h[t % 2][:, D:2 * D], lo, w1s[:, k, 0:D], start=False, stop=k == KC - 1)
                ins.then_inc(s_m1, 1)

            def filter_w_pair(i, q):
                if q == 0 and not later(i):
                    pe.wait_ge(s_setup, 1)
                pe.wait_ge(s_hlo, PAIRS * i + q + 1)
                if q >= 1 or later(i):
                    pe.wait_ge(s_fs, PAIRS * i + q)
                hi, lo = (m[:, q % 2, :, :].rearrange("p t d -> p (t d)") for m in (hid_hi, hid_lo))
                nc.tensor.matmul(ps_f[:, 0:2 * D], fw_hi[:], hi, start=True, stop=False)
                nc.tensor.matmul(ps_f[:, 0:2 * D], fw_lo[:], hi, start=False, stop=False)
                nc.tensor.matmul(ps_f[:, 0:2 * D], fw_hi[:], lo, start=False, stop=True).then_inc(s_f, 1)

            def corner_sums(i):
                pe.wait_ge(s_acc, PAIRS * (i + 1))
                pe.wait_ge(s_pre, TILES * (i + 1))
                nc.tensor.matmul(ps_corner[0:4, 0:D], corner_w[:], corner_acc[:], start=True, stop=True).then_inc(s_cmm, 1)

            def filter_h_chunk(i, c):
                banks = ps_y[c % 2]
                pe.wait_ge(s_cols_a[c], 16 * 2 * (i + 1))
                if c == 0:
                    pe.wait_ge(s_corner, i + 1)
                    pe.wait_ge(s_xlo, UNITS * (i + 1))
                elif c == 1:
                    pe.wait_ge(s_fs, PAIRS * (i + 1))
                    if later(i):
                        pe.wait_ge(s_add, HALVES * i - 4 + 1)
                elif c >= 2:
                    pe.wait_ge(s_yabs, YBANKS * CHUNKS * i + YBANKS * (c - 1))
                for v in range(2):
                    nc.tensor.matmul(banks[v][:], corner[:, 0:P], corner_hw[:], start=True, stop=False)
                    for m in range(4):
                        ins = nc.tensor.matmul(banks[v][:, m * P:(m + 1) * P], cols_a[:, CHUNK * c + 4 * v + m, :], fh[:],
                                               start=False, stop=m == 3)
                    ins.then_inc(s_y, 1)
                if c % 2 == 0:
                    pe.wait_ge(s_cols_b[c // 2], 16 * 4 * (i + 1))
                nc.tensor.matmul(banks[2][:], corner[:, P:2 * P], corner_hw[:], start=True, stop=False)
                for m in range(4):
                    ins = nc.tensor.matmul(banks[2][:, m * P:(m + 1) * P], cols_b[:, BMULS * c + m, :], fh[:],
                                           start=False, stop=m == 3)
                ins.then_inc(s_y, 1)

            def out_half(i, u):
                t, f = divmod(u, 2)
                r = t // 2
                if u == 0:
                    pe.wait_ge(s_add, HALVES * i + 1)
                elif u >= 3:
                    pe.wait_ge(s_add, HALVES * i + u - 2 + 1)
                o = ps_o[u % 3][:, 0:HALF]
                n = slice(f * HALF, (f + 1) * HALF)
                a_hi, a_lo, b, b1 = (m[:, r % 2, t % 2, :] for m in (oa_hi, oa_lo, ob, ob1))
                if u % 4 == 0:
                    pe.wait_ge(s_ahi, PAIRS * i + r + 1)
                nc.tensor.matmul(o, a_hi, w2a_hi[:, n], start=True, stop=False)
                nc.tensor.matmul(o, a_hi, w2a_lo[:, n], start=False, stop=False)
                if u % 4 == 0:
                    pe.wait_ge(s_b1, PAIRS * i + r + 1)
                nc.tensor.matmul(o, b1, w2b_lo[:, n], start=False, stop=False)
                if u % 4 == 0:
                    pe.wait_ge(s_alo, PAIRS * i + r + 1)
                nc.tensor.matmul(o, a_lo, w2a_hi[:, n], start=False, stop=False)
                if u % 4 == 0:
                    pe.wait_ge(s_blo, PAIRS * i + r + 1)
                nc.tensor.matmul(o, b, w2b_hi[:, n], start=False, stop=True).then_inc(s_o, 1)

            def turn(i, a, c):
                for q, r in steps(a, c):
                    for j in range(UPP):
                        if q is not None:
                            if q == 0 and j == 0:
                                for n in range(AHEAD):
                                    transpose_unit(i, n)
                            if unit_ahead(q, j) is not None:
                                transpose_unit(i, unit_ahead(q, j))
                            if q < PAIRS:
                                mm1_unit(i, UPP * q + j)
                            if q >= 1 and j == (2 if q == PAIRS else 1):
                                filter_w_pair(i, q - 1)
                        if r is not None:
                            for u in OUT_HALVES[j]:
                                out_half(i - 1, 4 * r + u)
                if a:
                    corner_sums(i)
                    for n in range(CHUNKS):
                        filter_h_chunk(i, n)
                    if c:
                        pe.wait_ge(s_yabs, YBANKS * CHUNKS * (i + 1))
                        for u in range(4):
                            out_half(i - 1, HALVES - 4 + u)

            turns(pe, turn)

        @block.scalar
        def _(act):
            def xt_hi_unit(i, n):
                act.wait_ge(s_t, UNITS * i + n + 1)
                if n >= XT_SLOTS or later(i):
                    act.wait_ge(s_m1, UNITS * i + n - XT_SLOTS + 1)
                nc.scalar.activation(xt_hi[:, n % XT_SLOTS, :], ps_xt[n % 2][:], ACT.Copy).then_inc(s_xhi, 1)

            def gelu_pair(i, q):
                act.wait_ge(s_pre, TILES * i + 2 * q + 2)
                if q >= 2 or later(i):
                    act.wait_ge(s_f, PAIRS * i + q - 1)
                pre = hid[:, q % 2, :, :]
                nc.scalar.activation(hid_hi[:, q % 2, :, :], pre, ACT.Gelu)
                nc.scalar.activation(pre, pre, ACT.Gelu).then_inc(s_gelu, 1)

            def stage_filtered(i, q):
                act.wait_ge(s_f, PAIRS * i + q + 1)
                if q >= 2 or later(i):
                    act.wait_ge(s_fw[q % 2], 16 * (PAIRS // 2 * i + q // 2))
                nc.scalar.activation(filt[:, q % 2, :, :].rearrange("p t d -> p (t d)"), ps_f[:, 0:2 * D], ACT.Copy).then_inc(s_fs, 1)

            def y_bank(i, c, v):
                act.wait_ge(s_y, YBANKS * CHUNKS * i + YBANKS * c + v + 1)
                if c == 0 and v == 0 and later(i):
                    act.wait_ge(s_blo, PAIRS * i)
                    act.wait_ge(s_b1, PAIRS * i)
                bank = ps_y[c % 2][v][:].rearrange("p (m n) -> p n m", m=4)
                if v < 2:
                    dst = ya[:].rearrange("p t (a n) -> p (t a) n", a=4)[:, :, CHUNK * c + 4 * v:CHUNK * c + 4 * v + 4]
                else:
                    dst = yb[:, :, BMULS * c:BMULS * (c + 1)]
                nc.scalar.activation(dst, bank, ACT.Abs).then_inc(s_yabs, 1)

            def split_hi_pair(i, r):
                if r == 0:
                    act.wait_ge(s_yabs, YBANKS * CHUNKS * (i + 1))
                elif r == 1:
                    act.wait_ge(s_o, HALVES * i + 1)
                else:
                    act.wait_ge(s_o, HALVES * i + 4 * (r - 1))
                nc.scalar.activation(oa_hi[:, r % 2, :, :], ya[:, 2 * r:2 * r + 2, :], ACT.Copy).then_inc(s_ahi, 1)
                hi, hi1, y = ob[:, r % 2, :, :], ob1[:, r % 2, :, :], yb_pair(r)
                nc.scalar.activation(quarters(hi, 0)[0:DB], y[0:DB], ACT.Copy)
                nc.scalar.activation(quarters(hi, 1)[DB:P], y[DB:P], ACT.Copy).then_inc(s_bhi, 1)
                nc.scalar.activation(quarters(hi1, 0)[0:DB], y[0:DB], ACT.Copy)
                nc.scalar.activation(quarters(hi1, 1)[0:DB], y[DB:P], ACT.Copy).then_inc(s_b1, 1)

            def turn(i, a, c):
                if c:
                    split_hi_pair(i - 1, 0)
                for q, r in steps(a, c):
                    for j in range(UPP):
                        if q is not None:
                            if q == 0 and j == 0:
                                for n in range(AHEAD):
                                    xt_hi_unit(i, n)
                            if unit_ahead(q, j) is not None:
                                xt_hi_unit(i, unit_ahead(q, j))
                            if q >= 1 and j == 0:
                                gelu_pair(i, q - 1)
                            if q >= 1 and j == 2:
                                stage_filtered(i, q - 1)
                        if r is not None and j == 0 and r + 1 < PAIRS:
                            split_hi_pair(i - 1, r + 1)
                if a:
                    for n in range(CHUNKS):
                        for v in range(YBANKS):
                            y_bank(i, n, v)

            turns(act, turn)

        @block.vector
        def _(dve):
            chain = [0]

            def link(ins):
                chain[0] += 1
                ins.then_inc(s_chain, 1)
                dve.wait_ge(s_chain, chain[0])

            w1f = x_tail[:, TAIL - 2:TAIL, :].rearrange("p t (k d) -> p (t k) d", d=D)[:, 0:KC, :]
            fwf, cornerf, w2af, w2bf, b2f = (x_tail[:, 0, 0:P], x_tail[:, 0, P:5 * P], x_tail[:, 1, :], x_tail[:, 2, :],
                                             x_tail[:, 3, :])
            dve.wait_ge(s_w1, 32)
            link(nc.vector.tensor_copy(w1s[:, :, 0:D], w1f))
            nc.vector.tensor_tensor(w1s[:, :, D:2 * D], w1f, w1s[:, :, 0:D].bitcast(F32), ALU.subtract).then_inc(s_w1s, 1)

            def set_up():
                dve.wait_ge(s_const, 16 * 9)
                nc.vector.memset(corner[:].bitcast(F32), 0.0)
                nc.vector.memset(w2b_lo[DB:P, :].bitcast(F32), 0.0)
                nc.vector.memset(ob1[DB:P, :, :, :].bitcast(F32), 1.0)
                nc.vector.tensor_copy(w2a_hi[:], w2af)
                nc.vector.tensor_copy(w2b_hi[:], w2bf)
                nc.vector.tensor_copy(corner_hw[:], cornerf)
                link(nc.vector.tensor_copy(fw_hi[:], fwf))
                nc.vector.tensor_tensor(w2a_lo[:], w2af, w2a_hi[:].bitcast(F32), ALU.subtract)
                nc.vector.tensor_tensor(w2b_lo[0:DB, :], w2bf[0:DB], w2b_hi[0:DB, :].bitcast(F32), ALU.subtract)
                nc.vector.tensor_tensor(fw_lo[:], fwf, fw_hi[:].bitcast(F32), ALU.subtract)
                nc.vector.tensor_copy(w2b_lo[DB:DB + 1, :], b2f[DB:DB + 1]).then_inc(s_add, 1)
                link(nc.vector.tensor_copy(w2b_lo[96:97, :], b2f[96:97]))
                nc.vector.tensor_tensor(w2b_lo[96:97, :], b2f[96:97], w2b_lo[96:97, :].bitcast(F32), ALU.subtract).then_inc(s_setup, 1)

            def xt_lo_unit(i, n):
                dve.wait_ge(s_xhi, UNITS * i + n + 1)
                nc.vector.tensor_tensor(xt_lo[:, n % XT_SLOTS, :], ps_xt[n % 2][:], xt_hi[:, n % XT_SLOTS, :].bitcast(F32),
                                        ALU.subtract).then_inc(s_xlo, 1)

            def hid_sum(i, t):
                dve.wait_ge(s_m1, UNITS * i + -(-KC * (t + 1) // BLOCKS))
                if t % 2 == 0 and (t >= 4 or later(i)):
                    dve.wait_ge(s_acc, PAIRS * i + t // 2 - 1)
                nc.vector.tensor_tensor(hid[:, t // 2 % 2, t % 2, :], ps_h[t % 2][:, D:2 * D], b1_rows[:], ALU.add).then_inc(s_sum, 1)

            def hid_pre(i, t):
                dve.wait_ge(s_sum, TILES * i + t + 1)
                h = hid[:, t // 2 % 2, t % 2, :]
                nc.vector.tensor_tensor(h, ps_h[t % 2][:, 0:D], h, ALU.add).then_inc(s_pre, 1)

            def hid_lo_pair(i, q):
                dve.wait_ge(s_gelu, PAIRS * i + q + 1)
                if q >= 2 or later(i):
                    dve.wait_ge(s_f, PAIRS * i + q - 1)
                nc.vector.tensor_tensor(hid_lo[:, q % 2, :, :], hid[:, q % 2, :, :], hid_hi[:, q % 2, :, :].bitcast(F32),
                                        ALU.subtract).then_inc(s_hlo, 1)

            def corner_split(i):
                dve.wait_ge(s_cmm, i + 1)
                nc.vector.tensor_copy(corner[0:4, 0:D], ps_corner[0:4, 0:D])
                nc.vector.tensor_copy(corner[0:4, D:2 * P], ps_corner[0:4, P:D]).then_inc(s_chi, 1)
                dve.wait_ge(s_chi, i + 1)
                nc.vector.tensor_tensor(corner[32:36, 0:D], ps_corner[0:4, 0:D], corner[0:4, 0:D].bitcast(F32), ALU.subtract)
                nc.vector.tensor_tensor(corner[32:36, D:2 * P], ps_corner[0:4, P:D], corner[0:4, D:2 * P].bitcast(F32),
                                        ALU.subtract).then_inc(s_corner, 1)

            def split_a_lo_pair(i, r):
                dve.wait_ge(s_ahi, PAIRS * i + r + 1)
                hi = oa_hi[:, r % 2, :, :].bitcast(F32)
                nc.vector.tensor_tensor(oa_lo[:, r % 2, :, :], ya[:, 2 * r:2 * r + 2, :], hi, ALU.subtract).then_inc(s_alo, 1)

            def split_b_lo_pair(i, r):
                dve.wait_ge(s_bhi, PAIRS * i + r + 1)
                o, y = ob[:, r % 2, :, :], yb_pair(r)
                for v, (own, other) in enumerate(((slice(0, DB), slice(DB, P)), (slice(DB, P), slice(0, DB)))):
                    m = quarters(o, v)
                    ins = nc.vector.tensor_tensor(m[other], y[own], m[own].bitcast(F32), ALU.subtract)
                ins.then_inc(s_blo, 1)

            def add_half(i, u):
                dve.wait_ge(s_o, HALVES * i + u + 1)
                t, f = divmod(u, 2)
                if t >= FIRST_TAIL and u % (2 * GROUP) == 0:
                    dve.wait_ge(s_x[t // GROUP], 16 * (i + 1))
                x_half = xs[:, t, f * HALF:(f + 1) * HALF]
                nc.vector.tensor_tensor(x_half, ps_o[u % 3][:, 0:HALF], x_half, ALU.add).then_inc(s_add, 1)

            def turn(i, a, c):
                if c:
                    split_a_lo_pair(i - 1, 0)
                    split_b_lo_pair(i - 1, 0)
                for q, r in steps(a, c):
                    for j in range(UPP):
                        if q is not None:
                            if q == 0 and j == 0:
                                for n in range(AHEAD):
                                    xt_lo_unit(i, n)
                                if not later(i):
                                    set_up()
                            if unit_ahead(q, j) is not None:
                                xt_lo_unit(i, unit_ahead(q, j))
                            if q >= 1 and j == 0:
                                hid_lo_pair(i, q - 1)
                            if q < PAIRS and j >= 1:
                                hid_sum(i, 2 * q + j - 1)
                                hid_pre(i, 2 * q + j - 1)
                        if r is not None:
                            add_half(i - 1, 4 * r + OUT_HALVES[j][0])
                            if j == 0 and r + 1 < PAIRS:
                                split_a_lo_pair(i - 1, r + 1)
                            if j == 1 and r + 1 < PAIRS:
                                split_b_lo_pair(i - 1, r + 1)
                            for u in OUT_HALVES[j][1:]:
                                add_half(i - 1, 4 * r + u)
                if a:
                    corner_split(i)
                    if c:
                        for u in range(4):
                            add_half(i - 1, HALVES - 4 + u)

            turns(dve, turn)

        @block.gpsimd
        def _(pool):
            def turn(i, a, c):
                if not a:
                    return
                for q in range(PAIRS):
                    pool.wait_ge(s_gelu, PAIRS * i + q + 1)
                    if q == 0:
                        if later(i):
                            pool.wait_ge(s_cmm, i)
                        nc.gpsimd.tensor_tensor(corner_acc[:], hid[:, 0, 0, :], hid[:, 0, 1, :], ALU.subtract).then_inc(s_acc, 1)
                        continue
                    pool.wait_ge(s_acc, PAIRS * i + q)
                    nc.gpsimd.tensor_tensor(diff[:], hid[:, q % 2, 0, :], hid[:, q % 2, 1, :], ALU.subtract).then_inc(s_diff, 1)
                    pool.wait_ge(s_diff, (PAIRS - 1) * i + q)
                    nc.gpsimd.tensor_tensor(corner_acc[:], corner_acc[:], diff[:], ALU.add).then_inc(s_acc, 1)

            turns(pool, turn)


def filters():
    import numpy as np

    n = np.arange(H)
    line = int((W * H * 0.25) ** 0.5 // 2)
    freq = np.arange(-line, line)
    d = n[:, None] - n[None, :]
    real = np.cos(2 * np.pi * freq[:, None, None] * d / H).sum(0) / H
    cos, sin = np.array([1, 0, -1, 0])[n % 4], np.array([0, 1, 0, -1])[n % 4]
    filter_w = np.kron(np.eye(2), real)
    filter_h = np.einsum("uv,hg->uhgv", np.eye(2), real).reshape(P, P)
    corner_in = np.zeros((2, W, 4))
    for a in range(2):
        corner_in[a, :, 2 * a] = cos / (H * W)
        corner_in[a, :, 2 * a + 1] = sin / (H * W)
    spread = np.zeros((P, 4, H, 2))
    for m in range(4):
        for w2 in range(2):
            terms = (-sin * sin[m], sin * cos[m], cos * sin[m], -cos * cos[m])
            for j, term in enumerate(terms):
                spread[j, m, :, w2] = spread[32 + j, m, :, w2] = term
    f = np.float32
    return {"identity": np.eye(P, dtype=f), "filter_w": filter_w.astype(f), "filter_h": filter_h.astype(f),
            "corner_in": corner_in.reshape(P, 4).astype(f), "corner_out": spread.reshape(P, 4 * P).astype(f)}


def kernel(x, L0_conv_W1, L0_conv_b1, L0_conv_W2, L0_conv_b2):
    import numpy as np
    import concourse.bacc as bacc
    from concourse.bass_utils import run_bass_kernel_spmd

    arrays = {
        "x": np.ascontiguousarray(x),
        "w1t": np.ascontiguousarray(np.asarray(L0_conv_W1).T),
        "b1": np.ascontiguousarray(L0_conv_b1),
        "w2t": np.ascontiguousarray(np.asarray(L0_conv_W2).T),
        "b2": np.ascontiguousarray(L0_conv_b2),
        **filters(),
    }
    nc = bacc.Bacc("TRN2", target_bir_lowering=False, num_devices=1, dynamic_dma_scratch_size=1024)
    aps = [nc.dram_tensor(f"{name}_dram", a.shape, mybir.dt.from_np(a.dtype), kind="ExternalInput").ap()
           for name, a in arrays.items()]
    out = nc.dram_tensor("out_dram", arrays["x"].shape, F32, kind="ExternalOutput").ap()
    lowpass_kernel(nc, *aps, out)
    result = run_bass_kernel_spmd(nc, [{f"{name}_dram": a for name, a in arrays.items()}], core_ids=[0])
    return result.results[0]["out_dram"]
```

```python
from contextlib import ExitStack

import concourse.bass as bass
from concourse import mybir

F32 = mybir.dt.float32
F32R = mybir.dt.float32r
I32 = mybir.dt.int32
ALU = mybir.AluOpType
ACT = mybir.ActivationFunctionType

P = 128
IMAGES, H, W, C, D = 16, 64, 64, 768, 192
KC = C // P
TILES = H * W // P
PAIRS = TILES // 2
GROUP = 4
GROUPS = TILES // GROUP
DB = D - P
HALF = C // 2

BLOCKS = 4
UNITS = TILES * KC // BLOCKS
UPP = UNITS // PAIRS
FIRST_LOADS = 2
XT_SLOTS = 4
AHEAD = 2

LAG = 8
TAIL = 2 * GROUP
TAIL_PAIRS = TAIL // 2
FIRST_TAIL = TILES - TAIL
MAIN_GROUPS = FIRST_TAIL // GROUP
TAIL_GROUPS = GROUPS - MAIN_GROUPS
FIRST_COPY = 3
TAIL_STEPS = 13, 14
FREE_HALVES = 4
HALVES = 2 * TILES

CHUNK = 8
CHUNKS = W // 2 // CHUNK
BCOLS = W // 4
BMULS = BCOLS // CHUNKS
YBANKS = 3


def lowpass_kernel(nc, x, w1t, b1, w2t, b2, identity, filter_w, filter_h, corner_in, corner_out, out):
    x_v = x.rearrange("b h w c -> b (h w) c").rearrange("b (t p) c -> b p t c", p=P)
    out_v = out.rearrange("b h w c -> b (h w) c").rearrange("b (t p) c -> b p t c", p=P)
    rows = nc.dram_tensor("filtered_rows", (H, W, D), F32, kind="Internal").ap()
    rows_in = rows.rearrange("(t a) w d -> (a w) t d", a=2)

    ctx = ExitStack()
    with ctx:
        def sb(name, shape, dt=F32):
            return ctx.enter_context(nc.sbuf_tensor(name, shape, dt))

        def sem(name):
            return ctx.enter_context(nc.semaphore(name))

        xs = sb("xs", [P, TILES, C])
        w1s = sb("w1s", [P, KC, 2 * D], F32R)
        w2a_hi = sb("w2a_hi", [P, C], F32R)
        w2a_lo = sb("w2a_lo", [P, C], F32R)
        w2b_hi = sb("w2b_hi", [P, C], F32R)
        w2b_lo = sb("w2b_lo", [P, C], F32R)
        ident = sb("ident", [P, P])
        b1_rows = sb("b1_rows", [P, D])
        fw_hi = sb("fw_hi", [P, P], F32R)
        fw_lo = sb("fw_lo", [P, P], F32R)
        fh = sb("fh", [P, P])
        corner_w = sb("corner_w", [P, 4])
        corner_hw = sb("corner_hw", [P, 4 * P], F32R)
        xt_hi = sb("xt_hi", [P, XT_SLOTS, BLOCKS * P], F32R)
        xt_lo = sb("xt_lo", [P, XT_SLOTS, BLOCKS * P], F32R)
        hid = sb("hid", [P, 2, 2, D])
        hid_hi = sb("hid_hi", [P, 2, 2, D], F32R)
        hid_lo = sb("hid_lo", [P, 2, 2, D], F32R)
        filt = sb("filt", [P, 2, 2, D])
        x_tail = sb("x_tail", [P, TAIL, C])
        cols_a = [m[:].bitcast(F32).rearrange("p s (m d) -> p (s m) d", d=P) for m in (xt_hi, xt_lo)]
        cols_b = sb("cols_b", [P, BCOLS, 2 * DB])
        diff = sb("diff", [P, D])
        corner_acc = sb("corner_acc", [P, D])
        corner = sb("corner", [P, 2 * P], F32R)
        ya = sb("ya", [P, TILES, P])
        yb = sb("yb", [P, 2 * H, BCOLS])
        oa_hi = sb("oa_hi", [P, 2, 2, P], F32R)
        oa_lo = sb("oa_lo", [P, 2, 2, P], F32R)
        ob = sb("ob", [P, 2, 2, P], F32R)
        ob1 = sb("ob1", [P, 2, 2, P], F32R)

        w1f = x_tail[:, TAIL - 2:TAIL, :].rearrange("p t (k d) -> p (t k) d", d=D)[:, 0:KC, :]
        fwf, cornerf, w2af, w2bf, b2f = (x_tail[:, 0, 0:P], x_tail[:, 0, P:5 * P], x_tail[:, 1, :], x_tail[:, 2, :],
                                         x_tail[:, 3, :])

        ps = [ctx.enter_context(nc.psum_tensor(f"ps{n}", [P, 512], F32)) for n in range(8)]
        ps_xt = ps[0:2]
        ps_h = ps[2:4]
        ps_f = ps[4]
        ps_o = [ps[6], ps[7], ps[5]]
        ps_corner = ps[3]
        ps_y = [ps[0:3], ps[3:6]]

        s_const = sem("const_loaded")
        s_ident = sem("ident_loaded")
        s_w1 = sem("w1_loaded")
        s_b1_rows = sem("b1_loaded")
        s_w1s = sem("w1_ready")
        s_w2_hi = sem("w2_hi_ready")
        s_setup = sem("setup_done")
        s_chain = sem("setup_chain")
        s_x = [sem(f"x_loaded{g}") for g in range(MAIN_GROUPS)]
        s_x_first = sem("x_first_pair_loaded")
        s_t = sem("transposed")
        s_xhi = sem("xt_hi_ready")
        s_xlo = sem("xt_lo_ready")
        s_m1 = sem("mm1_unit_done")
        s_sum = sem("hid_summed")
        s_pre = sem("hid_pre_ready")
        s_gelu = sem("gelu_done")
        s_hlo = sem("hid_lo_ready")
        s_f = sem("filtered_w")
        s_fs = sem("filtered_staged")
        s_fw = [sem(f"rows_written{n}") for n in range(2)]
        s_cols_a = [sem(f"cols_a_loaded{c}") for c in range(CHUNKS)]
        s_cols_b = [sem(f"cols_b_loaded{n}") for n in range(2)]
        s_diff = sem("corner_diff")
        s_acc = sem("corner_acc_done")
        s_cmm = sem("corner_sums_done")
        s_chi = sem("corner_hi_ready")
        s_corner = sem("corner_ready")
        s_y = sem("y_bank_done")
        s_yabs = sem("y_banks_stored_by_act")
        s_yabs_dve = sem("y_bank_stored_by_dve")
        s_ahi = sem("oa_hi_ready")
        s_bhi = sem("ob_hi_ready")
        s_alo = sem("oa_lo_ready")
        s_blo = sem("ob_lo_ready")
        s_b1 = sem("ob1_ready")
        s_xt = [sem(f"x_tail_loaded{n}") for n in range(TAIL_GROUPS)]
        s_o = sem("out_half_done")
        s_add = sem("out_half_added")
        s_out = [sem(f"stored{g}") for g in range(MAIN_GROUPS)]
        s_tail_out = sem("tail_stored")
        s_copied = sem("tail_tiles_copied")

        block = ctx.enter_context(nc.Block())

        def quarters(o, v):
            return o.rearrange("p t (n v m) -> p (t n) v m", v=2, m=BCOLS)[:, :, v, :]

        def yb_pair(r):
            return yb[:, 8 * r:8 * (r + 1), :]

        def later(i):
            return not isinstance(i, int) or i > 0

        def steps(a, c):
            if not a:
                return [(None, r) for r in range(PAIRS)]
            if not c:
                return [(q, None) for q in range(PAIRS + 1)]
            before = PAIRS - TAIL_PAIRS
            return ([(s - LAG if s >= LAG else None, s) for s in range(before)]
                    + [(q, None) for q in range(before - LAG, PAIRS)]
                    + [(PAIRS, before)] + [(None, r) for r in range(before + 1, PAIRS - 1)])

        def turns(eng, turn):
            turn(0, True, False)
            with eng.Fori(1, IMAGES) as i:
                turn(i, True, True)
            turn(IMAGES, False, True)

        def out_bank(u):
            return ps_o[u % 3] if u < HALVES - 1 else ps_y[0][0]

        def starts(a, c, s, j):
            return a and ((s, j) == (LAG - 1, 1) if c else (s, j) == (0, 0))

        def y_in_bank(c, v):
            return ps_y[c % 2][v][:].rearrange("p (m n) -> p n m", m=4)

        def y_slot(c, v):
            if v < 2:
                m = CHUNK * c + 4 * v
                return ya[:].rearrange("p t (a n) -> p (t a) n", a=4)[:, :, m:m + 4]
            return yb[:, :, BMULS * c:BMULS * (c + 1)]

        def unit_ahead(q, j):
            n = UPP * q + j + AHEAD
            return n if n < UNITS else None

        def x_tile(t):
            return xs[:, t, :] if t < FIRST_TAIL else x_tail[:, t - FIRST_TAIL, :]

        OUT_HALVES = [(0, 1), (2,), (3,)]

        @block.sync
        def _(sp):
            def const(dst, src, s=s_const):
                sp.dma_start(dst, src).then_inc(s, 16)

            const(ident[:], identity, s_ident)
            const(w1f, w1t.rearrange("(k p) d -> p k d", p=P), s_w1)

            def load_constants():
                const(fwf, filter_w)
                const(cornerf, corner_out)
                const(fh[:], filter_h)
                const(corner_w[:], corner_in)
                const(w2af, w2t[0:P, :])
                for r in range(2):
                    const(w2bf[r * DB:(r + 1) * DB], w2t[P:D, :])
                for r in (64, 96):
                    const(b2f[r:r + 1], b2.rearrange("(a c) -> a c", a=1))

            def load_x(i, g):
                if later(i):
                    sp.wait_ge(s_out[g], 16 * i)
                first = GROUP * g
                if g == 0:
                    first = 2
                    sp.dma_start(xs[:, 0:2, :], x_v[i, :, 0:2, :]).then_inc(s_x_first, 16)
                    if not later(i):
                        const(b1_rows[:], b1.partition_broadcast(P), s_b1_rows)
                sp.dma_start(xs[:, first:GROUP * (g + 1), :], x_v[i, :, first:GROUP * (g + 1), :]).then_inc(s_x[g], 16)

            def load_x_tail(i, n):
                if later(i):
                    sp.wait_ge(s_copied, TAIL * i)
                else:
                    sp.wait_ge(s_setup, 2)
                sp.dma_start(x_tail[:, GROUP * n:GROUP * (n + 1), :],
                             x_v[i, :, FIRST_TAIL + GROUP * n:FIRST_TAIL + GROUP * (n + 1), :]).then_inc(s_xt[n], 16)

            def store(i, g):
                sp.wait_ge(s_add, HALVES * i + 2 * GROUP * (g + 1) + FREE_HALVES)
                s_stored = s_out[g] if g < MAIN_GROUPS else s_tail_out
                sp.dma_start(out_v[i, :, GROUP * g:GROUP * (g + 1), :], xs[:, GROUP * g:GROUP * (g + 1), :]).then_inc(s_stored, 16)

            def store_last_tile(t):
                sp.wait_ge(s_add, HALVES * (IMAGES - 1) + 2 * (t + 1) + FREE_HALVES)
                sp.dma_start(out_v[IMAGES - 1, :, t, :], xs[:, t, :]).then_inc(s_tail_out, 16)

            def write_rows(i, q):
                sp.wait_ge(s_fs, PAIRS * i + q + 1)
                sp.dma_start(rows_in[:, 2 * q:2 * q + 2, :], filt[:, q % 2, :, :]).then_inc(s_fw[q % 2], 16)

            def read_cols_a(i, c):
                if c == 0:
                    for n in range(2):
                        sp.wait_ge(s_fw[n], 16 * PAIRS // 2 * (i + 1))
                for w2 in range(2):
                    wc = w2 * W // 2 + CHUNK * c
                    n = CHUNK * (c % 2)
                    sp.dma_start(cols_a[c // 2][w2 * H:(w2 + 1) * H, n:n + CHUNK, :],
                                 rows[:, wc:wc + CHUNK, 0:P]).then_inc(s_cols_a[c], 16)

            def read_cols_b(i, n):
                for w2 in range(2):
                    for v in range(2):
                        wc = w2 * W // 2 + v * BCOLS + n * BCOLS // 2
                        sp.dma_start(cols_b[w2 * H:(w2 + 1) * H, n * BCOLS // 2:(n + 1) * BCOLS // 2, v * DB:(v + 1) * DB],
                                     rows[:, wc:wc + BCOLS // 2, P:D]).then_inc(s_cols_b[n], 16)

            def turn(i, a, c):
                if not c:
                    load_x(i, 0)
                    load_constants()
                    for g in range(1, FIRST_LOADS):
                        load_x(i, g)
                for s, (q, r) in enumerate(steps(a, c)):
                    if r is not None and r % 2 == 1 and r < (PAIRS - 3 if a else PAIRS - 1):
                        store(i - 1, r // 2)
                    if q is not None and q >= 1:
                        write_rows(i, q - 1)
                    if not c and s % 2 == 0:
                        g = FIRST_LOADS + s // 2
                        if g < MAIN_GROUPS:
                            load_x(i, g)
                        elif g < GROUPS:
                            load_x_tail(i, g - MAIN_GROUPS)
                    if a and c and s % 2 == 0 and 2 <= s <= PAIRS - TAIL_PAIRS:
                        load_x(i, s // 2 - 1)
                    if a and c and s in TAIL_STEPS:
                        load_x_tail(i, TAIL_STEPS.index(s))
                if a:
                    for n in range(2):
                        read_cols_a(i, 2 * n)
                        read_cols_b(i, n)
                        read_cols_a(i, 2 * n + 1)
                    if c:
                        store(i - 1, GROUPS - 2)
                        store(i - 1, GROUPS - 1)
                else:
                    for t in range(TILES - GROUP, TILES):
                        store_last_tile(t)

            turns(sp, turn)
            for g in range(MAIN_GROUPS):
                sp.wait_ge(s_out[g], 16 * IMAGES)
            sp.wait_ge(s_tail_out, 16 * (TAIL_GROUPS * IMAGES + GROUP - 1) + 1)
            for n in range(2):
                sp.wait_ge(s_fw[n], 16 * PAIRS // 2 * IMAGES)

        @block.tensor
        def _(pe):
            pe.wait_ge(s_ident, 16)

            def transpose_unit(i, n):
                if n == 0:
                    pe.wait_ge(s_x_first, 16 * (i + 1))
                elif n * BLOCKS == 2 * KC:
                    pe.wait_ge(s_x[0], 16 * (i + 1))
                elif n * BLOCKS % (GROUP * KC) == 0:
                    g = n * BLOCKS // (GROUP * KC)
                    if g < MAIN_GROUPS:
                        pe.wait_ge(s_x[g], 16 * (i + 1))
                    else:
                        pe.wait_ge(s_xt[g - MAIN_GROUPS], 16 * (i + 1))
                if n >= 2:
                    pe.wait_ge(s_xlo, UNITS * i + n - 1)
                elif n == 0 and later(i):
                    pe.wait_ge(s_yabs, 2 * CHUNKS * i)
                    pe.wait_ge(s_yabs_dve, CHUNKS * i)
                for b in range(BLOCKS):
                    t, k = divmod(BLOCKS * n + b, KC)
                    ins = nc.tensor.transpose(ps_xt[n % 2][:, b * P:(b + 1) * P], x_tile(t)[:, k * P:(k + 1) * P], ident[:])
                ins.then_inc(s_t, 1)

            def mm1_unit(i, n):
                if n == 0 and not later(i):
                    pe.wait_ge(s_w1s, 1)
                pe.wait_ge(s_xlo, UNITS * i + n + 1)
                for b in range(BLOCKS):
                    t, k = divmod(BLOCKS * n + b, KC)
                    if k == 0 and (t >= 2 or later(i)):
                        pe.wait_ge(s_pre, TILES * i + t - 1)
                    hi = xt_hi[:, n % XT_SLOTS, b * P:(b + 1) * P]
                    lo = xt_lo[:, n % XT_SLOTS, b * P:(b + 1) * P]
                    nc.tensor.matmul(ps_h[t % 2][:, 0:2 * D], hi, w1s[:, k, :], start=k == 0, stop=False)
                    ins = nc.tensor.matmul(ps_h[t % 2][:, D:2 * D], lo, w1s[:, k, 0:D], start=False, stop=k == KC - 1)
                ins.then_inc(s_m1, 1)

            def filter_w_pair(i, q):
                if q == 0 and not later(i):
                    pe.wait_ge(s_setup, 1)
                pe.wait_ge(s_hlo, PAIRS * i + q + 1)
                if q >= 1 or later(i):
                    pe.wait_ge(s_fs, PAIRS * i + q)
                hi, lo = (m[:, q % 2, :, :].rearrange("p t d -> p (t d)") for m in (hid_hi, hid_lo))
                nc.tensor.matmul(ps_f[:, 0:2 * D], fw_hi[:], hi, start=True, stop=False)
                nc.tensor.matmul(ps_f[:, 0:2 * D], fw_lo[:], hi, start=False, stop=False)
                nc.tensor.matmul(ps_f[:, 0:2 * D], fw_hi[:], lo, start=False, stop=True).then_inc(s_f, 1)

            def corner_sums(i):
                pe.wait_ge(s_acc, PAIRS * (i + 1))
                pe.wait_ge(s_pre, TILES * (i + 1))
                nc.tensor.matmul(ps_corner[0:4, 0:D], corner_w[:], corner_acc[:], start=True, stop=True).then_inc(s_cmm, 1)

            def filter_h_chunk(i, c):
                banks = ps_y[c % 2]
                pe.wait_ge(s_cols_a[c], 16 * 2 * (i + 1))
                if c == 0:
                    pe.wait_ge(s_corner, i + 1)
                    pe.wait_ge(s_xlo, UNITS * (i + 1))
                elif c == 1:
                    pe.wait_ge(s_fs, PAIRS * (i + 1))
                    if later(i):
                        pe.wait_ge(s_add, HALVES * i - 4 + FREE_HALVES)
                elif c >= 2:
                    pe.wait_ge(s_yabs, 2 * CHUNKS * i + 2 * (c - 1))
                    pe.wait_ge(s_yabs_dve, CHUNKS * i + c - 1)
                for v in range(2):
                    nc.tensor.matmul(banks[v][:], corner[:, 0:P], corner_hw[:], start=True, stop=False)
                    for m in range(4):
                        ins = nc.tensor.matmul(banks[v][:, m * P:(m + 1) * P], cols_a[c // 2][:, CHUNK * (c % 2) + 4 * v + m, :], fh[:],
                                               start=False, stop=m == 3)
                    ins.then_inc(s_y, 1)
                if c % 2 == 0:
                    pe.wait_ge(s_cols_b[c // 2], 16 * 4 * (i + 1))
                nc.tensor.matmul(banks[2][:], corner[:, P:2 * P], corner_hw[:], start=True, stop=False)
                for m in range(4):
                    ins = nc.tensor.matmul(banks[2][:, m * P:(m + 1) * P], cols_b[:, BMULS * c + m, :], fh[:],
                                           start=False, stop=m == 3)
                ins.then_inc(s_y, 1)

            def out_half(i, u):
                t, f = divmod(u, 2)
                r = t // 2
                if u < 3:
                    pe.wait_ge(s_add, HALVES * i + u - 3 + FREE_HALVES)
                elif u < HALVES - 1:
                    pe.wait_ge(s_add, HALVES * i + u - 2 + FREE_HALVES)
                o = out_bank(u)[:, 0:HALF]
                n = slice(f * HALF, (f + 1) * HALF)
                a_hi, a_lo, b, b1 = (m[:, r % 2, t % 2, :] for m in (oa_hi, oa_lo, ob, ob1))
                if u % 4 == 0:
                    pe.wait_ge(s_ahi, PAIRS * i + r + 1)
                nc.tensor.matmul(o, a_hi, w2a_hi[:, n], start=True, stop=False)
                nc.tensor.matmul(o, a_hi, w2a_lo[:, n], start=False, stop=False)
                if u % 4 == 0:
                    pe.wait_ge(s_b1, PAIRS * i + r + 1)
                nc.tensor.matmul(o, b1, w2b_lo[:, n], start=False, stop=False)
                if u % 4 == 0:
                    pe.wait_ge(s_alo, PAIRS * i + r + 1)
                nc.tensor.matmul(o, a_lo, w2a_hi[:, n], start=False, stop=False)
                if u % 4 == 0:
                    pe.wait_ge(s_blo, PAIRS * i + r + 1)
                nc.tensor.matmul(o, b, w2b_hi[:, n], start=False, stop=True).then_inc(s_o, 1)

            def turn(i, a, c):
                plan = steps(a, c)
                for s, (q, r) in enumerate(plan):
                    for j in range(UPP):
                        if starts(a, c, s, j):
                            for n in range(AHEAD):
                                transpose_unit(i, n)
                        if q is not None:
                            if unit_ahead(q, j) is not None:
                                transpose_unit(i, unit_ahead(q, j))
                            if q < PAIRS:
                                mm1_unit(i, UPP * q + j)
                            if q >= 1 and j == (2 if q == PAIRS else 1):
                                filter_w_pair(i, q - 1)
                        if r is not None:
                            for u in OUT_HALVES[j]:
                                out_half(i - 1, 4 * r + u)
                        if a and s == len(plan) - 1 and j == (0 if c else UPP - 1):
                            corner_sums(i)
                if a:
                    for n in range(CHUNKS):
                        filter_h_chunk(i, n)
                    if c:
                        for u in range(HALVES - 4, HALVES):
                            if out_bank(u) is ps_y[1][2]:
                                pe.wait_ge(s_yabs, 2 * CHUNKS * (i + 1))
                            out_half(i - 1, u)

            turns(pe, turn)

        @block.scalar
        def _(act):
            def set_up_hi(q):
                if q == 1:
                    act.wait_ge(s_const, 16 * 9)
                    nc.scalar.activation(w2a_hi[:], w2af, ACT.Copy).then_inc(s_w2_hi, 1)
                elif q == 2:
                    nc.scalar.activation(w2b_hi[:], w2bf, ACT.Copy).then_inc(s_w2_hi, 1)
                else:
                    nc.scalar.activation(corner_hw[:], cornerf, ACT.Copy)

            def xt_hi_unit(i, n):
                act.wait_ge(s_t, UNITS * i + n + 1)
                if n >= XT_SLOTS or later(i):
                    act.wait_ge(s_m1, UNITS * i + n - XT_SLOTS + 1)
                nc.scalar.activation(xt_hi[:, n % XT_SLOTS, :], ps_xt[n % 2][:], ACT.Copy).then_inc(s_xhi, 1)

            def gelu_pair(i, q):
                act.wait_ge(s_pre, TILES * i + 2 * q + 2)
                if q >= 2 or later(i):
                    act.wait_ge(s_f, PAIRS * i + q - 1)
                pre = hid[:, q % 2, :, :]
                nc.scalar.activation(hid_hi[:, q % 2, :, :], pre, ACT.Gelu)
                nc.scalar.activation(pre, pre, ACT.Gelu).then_inc(s_gelu, 1)

            def stage_filtered(i, q):
                act.wait_ge(s_f, PAIRS * i + q + 1)
                if q >= 2 or later(i):
                    act.wait_ge(s_fw[q % 2], 16 * (PAIRS // 2 * i + q // 2))
                nc.scalar.activation(filt[:, q % 2, :, :].rearrange("p t d -> p (t d)"), ps_f[:, 0:2 * D], ACT.Copy).then_inc(s_fs, 1)

            def y_bank(i, c, v):
                act.wait_ge(s_y, YBANKS * CHUNKS * i + YBANKS * c + v + 1)
                if c == 0 and v == 0 and later(i):
                    act.wait_ge(s_blo, PAIRS * i)
                    act.wait_ge(s_b1, PAIRS * i)
                nc.scalar.activation(y_slot(c, v), y_in_bank(c, v), ACT.Abs).then_inc(s_yabs, 1)

            def split_hi_pair(i, r):
                if r == 0:
                    act.wait_ge(s_yabs, 2 * CHUNKS * (i + 1))
                    act.wait_ge(s_yabs_dve, CHUNKS * (i + 1))
                elif r == 1:
                    act.wait_ge(s_o, HALVES * i + 1)
                else:
                    act.wait_ge(s_o, HALVES * i + 4 * (r - 1))
                nc.scalar.activation(oa_hi[:, r % 2, :, :], ya[:, 2 * r:2 * r + 2, :], ACT.Copy).then_inc(s_ahi, 1)
                hi, hi1, y = ob[:, r % 2, :, :], ob1[:, r % 2, :, :], yb_pair(r)
                nc.scalar.activation(quarters(hi, 0)[0:DB], y[0:DB], ACT.Copy)
                nc.scalar.activation(quarters(hi, 1)[DB:P], y[DB:P], ACT.Copy).then_inc(s_bhi, 1)
                nc.scalar.activation(quarters(hi1, 0)[0:DB], y[0:DB], ACT.Copy)
                nc.scalar.activation(quarters(hi1, 1)[0:DB], y[DB:P], ACT.Copy).then_inc(s_b1, 1)

            def copy_tail_tile(i, t):
                if t == 0:
                    act.wait_ge(s_tail_out, 16 * TAIL_GROUPS * i + 1)
                nc.scalar.activation(xs[:, FIRST_TAIL + t, :], x_tail[:, t, :], ACT.Copy).then_inc(s_copied, 1)

            def turn(i, a, c):
                for s, (q, r) in enumerate(steps(a, c)):
                    for j in range(UPP):
                        if starts(a, c, s, j):
                            for n in range(AHEAD):
                                xt_hi_unit(i, n)
                        if q is not None:
                            if unit_ahead(q, j) is not None:
                                xt_hi_unit(i, unit_ahead(q, j))
                            if q >= 1 and j == 0:
                                gelu_pair(i, q - 1)
                            if q >= 1 and j == 2:
                                stage_filtered(i, q - 1)
                            if not c and q in (1, 2, 3) and j == 2:
                                set_up_hi(q)
                        if r is not None and j == 0 and r + 1 < PAIRS:
                            split_hi_pair(i - 1, r + 1)
                        if c and j == 2 and FIRST_COPY <= s < FIRST_COPY + TAIL // 2:
                            for t in range(2):
                                copy_tail_tile(i - 1, 2 * (s - FIRST_COPY) + t)
                if a:
                    for n in range(CHUNKS):
                        y_bank(i, n, 0)
                        y_bank(i, n, 2)
                    split_hi_pair(i, 0)

            turns(act, turn)

        @block.vector
        def _(dve):
            chain = [0]

            def link(ins):
                chain[0] += 1
                ins.then_inc(s_chain, 1)
                dve.wait_ge(s_chain, chain[0])

            dve.wait_ge(s_w1, 16)
            link(nc.vector.tensor_copy(w1s[:, :, 0:D], w1f))
            nc.vector.tensor_tensor(w1s[:, :, D:2 * D], w1f, w1s[:, :, 0:D].bitcast(F32), ALU.subtract).then_inc(s_w1s, 1)

            def set_up_filters():
                dve.wait_ge(s_const, 16 * 9)
                nc.vector.memset(corner[:].bitcast(F32), 0.0)
                link(nc.vector.tensor_copy(fw_hi[:], fwf))
                nc.vector.tensor_tensor(fw_lo[:], fwf, fw_hi[:].bitcast(F32), ALU.subtract).then_inc(s_setup, 1)

            def set_up_w2():
                nc.vector.memset(w2b_lo[DB:P, :].bitcast(F32), 0.0).then_inc(s_tail_out, 1)
                nc.vector.memset(ob1[DB:P, :, :, :].bitcast(F32), 1.0)

            def set_up_w2a_lo():
                dve.wait_ge(s_w2_hi, 2)
                nc.vector.tensor_tensor(w2a_lo[:], w2af, w2a_hi[:].bitcast(F32), ALU.subtract)

            def set_up_w2b_lo():
                nc.vector.tensor_tensor(w2b_lo[0:DB, :], w2bf[0:DB], w2b_hi[0:DB, :].bitcast(F32), ALU.subtract)

            def set_up_b2_hi():
                nc.vector.tensor_copy(w2b_lo[DB:DB + 1, :], b2f[DB:DB + 1]).then_inc(s_add, FREE_HALVES)

            def set_up_b2_lo():
                link(nc.vector.tensor_copy(w2b_lo[96:97, :], b2f[96:97]))

            def set_up_b2_lo_rest():
                nc.vector.tensor_tensor(w2b_lo[96:97, :], b2f[96:97], w2b_lo[96:97, :].bitcast(F32), ALU.subtract).then_inc(s_setup, 1)

            def xt_lo_unit(i, n):
                dve.wait_ge(s_xhi, UNITS * i + n + 1)
                nc.vector.tensor_tensor(xt_lo[:, n % XT_SLOTS, :], ps_xt[n % 2][:], xt_hi[:, n % XT_SLOTS, :].bitcast(F32),
                                        ALU.subtract).then_inc(s_xlo, 1)

            def hid_sum(i, t):
                dve.wait_ge(s_m1, UNITS * i + -(-KC * (t + 1) // BLOCKS))
                if t == 0 and not later(i):
                    dve.wait_ge(s_b1_rows, 16)
                if t % 2 == 0 and (t >= 4 or later(i)):
                    dve.wait_ge(s_acc, PAIRS * i + t // 2 - 1)
                nc.vector.tensor_tensor(hid[:, t // 2 % 2, t % 2, :], ps_h[t % 2][:, D:2 * D], b1_rows[:], ALU.add).then_inc(s_sum, 1)

            def hid_pre(i, t):
                dve.wait_ge(s_sum, TILES * i + t + 1)
                h = hid[:, t // 2 % 2, t % 2, :]
                nc.vector.tensor_tensor(h, ps_h[t % 2][:, 0:D], h, ALU.add).then_inc(s_pre, 1)

            def hid_lo_pair(i, q):
                dve.wait_ge(s_gelu, PAIRS * i + q + 1)
                if q >= 2 or later(i):
                    dve.wait_ge(s_f, PAIRS * i + q - 1)
                nc.vector.tensor_tensor(hid_lo[:, q % 2, :, :], hid[:, q % 2, :, :], hid_hi[:, q % 2, :, :].bitcast(F32),
                                        ALU.subtract).then_inc(s_hlo, 1)

            def corner_split(i):
                dve.wait_ge(s_cmm, i + 1)
                nc.vector.tensor_copy(corner[0:4, 0:D], ps_corner[0:4, 0:D])
                nc.vector.tensor_copy(corner[0:4, D:2 * P], ps_corner[0:4, P:D]).then_inc(s_chi, 1)
                dve.wait_ge(s_chi, i + 1)
                nc.vector.tensor_tensor(corner[32:36, 0:D], ps_corner[0:4, 0:D], corner[0:4, 0:D].bitcast(F32), ALU.subtract)
                nc.vector.tensor_tensor(corner[32:36, D:2 * P], ps_corner[0:4, P:D], corner[0:4, D:2 * P].bitcast(F32),
                                        ALU.subtract).then_inc(s_corner, 1)

            def y_bank_dve(i, c):
                dve.wait_ge(s_y, YBANKS * CHUNKS * i + YBANKS * c + 2)
                if c == 0 and later(i):
                    dve.wait_ge(s_blo, PAIRS * i)
                nc.vector.tensor_scalar(y_slot(c, 1).bitcast(I32), y_in_bank(c, 1).bitcast(I32), 0x7FFFFFFF, None,
                                        ALU.bitwise_and).then_inc(s_yabs_dve, 1)

            def split_a_lo_pair(i, r):
                dve.wait_ge(s_ahi, PAIRS * i + r + 1)
                hi = oa_hi[:, r % 2, :, :].bitcast(F32)
                nc.vector.tensor_tensor(oa_lo[:, r % 2, :, :], ya[:, 2 * r:2 * r + 2, :], hi, ALU.subtract).then_inc(s_alo, 1)

            def split_b_lo_pair(i, r):
                dve.wait_ge(s_bhi, PAIRS * i + r + 1)
                o, y = ob[:, r % 2, :, :], yb_pair(r)
                for v, (own, other) in enumerate(((slice(0, DB), slice(DB, P)), (slice(DB, P), slice(0, DB)))):
                    m = quarters(o, v)
                    ins = nc.vector.tensor_tensor(m[other], y[own], m[own].bitcast(F32), ALU.subtract)
                ins.then_inc(s_blo, 1)

            def add_half(i, u):
                dve.wait_ge(s_o, HALVES * i + u + 1)
                t, f = divmod(u, 2)
                if t >= FIRST_TAIL and f == 0:
                    dve.wait_ge(s_copied, TAIL * i + t - FIRST_TAIL + 1)
                x_half = xs[:, t, f * HALF:(f + 1) * HALF]
                nc.vector.tensor_tensor(x_half, out_bank(u)[:, 0:HALF], x_half, ALU.add).then_inc(s_add, 1)

            def turn(i, a, c):
                set_up_at = {(0, 2): set_up_filters, (1, 2): set_up_w2, (3, 2): set_up_w2a_lo, (4, 2): set_up_w2b_lo,
                             (5, 2): set_up_b2_hi, (6, 2): set_up_b2_lo, (7, 2): set_up_b2_lo_rest}
                plan = steps(a, c)
                for s, (q, r) in enumerate(plan):
                    for j in range(UPP):
                        if starts(a, c, s, j):
                            for n in range(AHEAD):
                                xt_lo_unit(i, n)
                        if q is not None:
                            if unit_ahead(q, j) is not None:
                                xt_lo_unit(i, unit_ahead(q, j))
                            if q >= 1 and j == 0:
                                hid_lo_pair(i, q - 1)
                            if q < PAIRS and j >= 1:
                                hid_sum(i, 2 * q + j - 1)
                                hid_pre(i, 2 * q + j - 1)
                            if not c and (q, j) in set_up_at:
                                set_up_at[q, j]()
                        if a and s == len(plan) - 1 and j == (1 if c else UPP - 1):
                            corner_split(i)
                        if r is not None:
                            add_half(i - 1, 4 * r + OUT_HALVES[j][0])
                            if j == 0 and r + 1 < PAIRS:
                                split_a_lo_pair(i - 1, r + 1)
                            if j == 1 and r + 1 < PAIRS:
                                split_b_lo_pair(i - 1, r + 1)
                            for u in OUT_HALVES[j][1:]:
                                add_half(i - 1, 4 * r + u)
                if a:
                    for n in range(CHUNKS):
                        y_bank_dve(i, n)
                    if c:
                        add_half(i - 1, HALVES - 4)
                        add_half(i - 1, HALVES - 3)
                    split_a_lo_pair(i, 0)
                    split_b_lo_pair(i, 0)
                    if c:
                        add_half(i - 1, HALVES - 2)
                        add_half(i - 1, HALVES - 1)

            turns(dve, turn)

        @block.gpsimd
        def _(pool):
            def turn(i, a, c):
                if not a:
                    return
                for q in range(PAIRS):
                    pool.wait_ge(s_gelu, PAIRS * i + q + 1)
                    if q == 0:
                        if later(i):
                            pool.wait_ge(s_cmm, i)
                        nc.gpsimd.tensor_tensor(corner_acc[:], hid[:, 0, 0, :], hid[:, 0, 1, :], ALU.subtract).then_inc(s_acc, 1)
                        continue
                    pool.wait_ge(s_acc, PAIRS * i + q)
                    nc.gpsimd.tensor_tensor(diff[:], hid[:, q % 2, 0, :], hid[:, q % 2, 1, :], ALU.subtract).then_inc(s_diff, 1)
                    pool.wait_ge(s_diff, (PAIRS - 1) * i + q)
                    nc.gpsimd.tensor_tensor(corner_acc[:], corner_acc[:], diff[:], ALU.add).then_inc(s_acc, 1)

            turns(pool, turn)


def filters():
    import numpy as np

    n = np.arange(H)
    line = int((W * H * 0.25) ** 0.5 // 2)
    freq = np.arange(-line, line)
    d = n[:, None] - n[None, :]
    real = np.cos(2 * np.pi * freq[:, None, None] * d / H).sum(0) / H
    cos, sin = np.array([1, 0, -1, 0])[n % 4], np.array([0, 1, 0, -1])[n % 4]
    filter_w = np.kron(np.eye(2), real)
    filter_h = np.einsum("uv,hg->uhgv", np.eye(2), real).reshape(P, P)
    corner_in = np.zeros((2, W, 4))
    for a in range(2):
        corner_in[a, :, 2 * a] = cos / (H * W)
        corner_in[a, :, 2 * a + 1] = sin / (H * W)
    spread = np.zeros((P, 4, H, 2))
    for m in range(4):
        for w2 in range(2):
            terms = (-sin * sin[m], sin * cos[m], cos * sin[m], -cos * cos[m])
            for j, term in enumerate(terms):
                spread[j, m, :, w2] = spread[32 + j, m, :, w2] = term
    f = np.float32
    return {"identity": np.eye(P, dtype=f), "filter_w": filter_w.astype(f), "filter_h": filter_h.astype(f),
            "corner_in": corner_in.reshape(P, 4).astype(f), "corner_out": spread.reshape(P, 4 * P).astype(f)}


def kernel(x, L0_conv_W1, L0_conv_b1, L0_conv_W2, L0_conv_b2):
    import numpy as np
    import concourse.bacc as bacc
    from concourse.bass_utils import run_bass_kernel_spmd

    arrays = {
        "x": np.ascontiguousarray(x),
        "w1t": np.ascontiguousarray(np.asarray(L0_conv_W1).T),
        "b1": np.ascontiguousarray(L0_conv_b1),
        "w2t": np.ascontiguousarray(np.asarray(L0_conv_W2).T),
        "b2": np.ascontiguousarray(L0_conv_b2),
        **filters(),
    }
    nc = bacc.Bacc("TRN2", target_bir_lowering=False, num_devices=1, dynamic_dma_scratch_size=1024)
    aps = [nc.dram_tensor(f"{name}_dram", a.shape, mybir.dt.from_np(a.dtype), kind="ExternalInput").ap()
           for name, a in arrays.items()]
    out = nc.dram_tensor("out_dram", arrays["x"].shape, F32, kind="ExternalOutput").ap()
    lowpass_kernel(nc, *aps, out)
    result = run_bass_kernel_spmd(nc, [{f"{name}_dram": a for name, a in arrays.items()}], core_ids=[0])
    return result.results[0]["out_dram"]
```
